# Optimizing a Trainium2 kernel written in Bass

```python
import numpy as np
import jax
import jax.numpy as jnp

def _softmax(x, axis=-1):
    return jax.nn.softmax(x, axis=axis)

def _gelu(x):
    return jax.nn.gelu(x, approximate=True)

def _silu(x):
    return jax.nn.silu(x)

def _sigmoid(x):
    return jax.nn.sigmoid(x)

def _layernorm(x, axis=-1, eps=1e-05):
    m = jnp.mean(x, axis=axis, keepdims=True)
    v = jnp.var(x, axis=axis, keepdims=True)
    return (x - m) / jnp.sqrt(v + eps)

def _scatter_add(tgt, idx, src, axis=0):
    return tgt.at[idx].add(src)

def _segment_sum(src, seg, n):
    return jax.ops.segment_sum(src, seg, n)
kernel_name = 'mk_seq_preln_d1_jaxref_r8_2db59b'

def setup_inputs(seed: int=0):
    np.random.seed(seed)
    _w = jnp.asarray

    def _L0_attn_setup():
        import jax, jax.numpy as jnp
        import numpy as np
        EMBED_DIM = 128
        key = jax.random.key(seed)
        ks = jax.random.split(key, 9)
        B, S, D = (4, 512, EMBED_DIM)
        s = 1.0 / np.sqrt(D)
        inp = {'x': jax.random.normal(ks[0], (B, S, D), dtype=jnp.float32)}
        names = ['q', 'k', 'v', 'out']
        for i, n in enumerate(names):
            inp[f'w_{n}'] = jax.random.uniform(ks[1 + 2 * i], (D, D), jnp.float32, -s, s)
            inp[f'b_{n}'] = jax.random.uniform(ks[2 + 2 * i], (D,), jnp.float32, -s, s)
        return inp
    _L0_attn_in = _L0_attn_setup()

    def _L0_ffn_setup():
        import jax, jax.numpy as jnp
        import numpy as np
        B, S, H, I, E = (2, 512, 128, 64, 8)
        key = jax.random.key(seed)
        ks = jax.random.split(key, 5)
        scale_h = 1.0 / np.sqrt(H)
        scale_i = 1.0 / np.sqrt(I)
        return {'hidden_states': jax.random.normal(ks[0], (B, S, H), dtype=jnp.float32), 'gate_w': jax.random.normal(ks[1], (E, H), dtype=jnp.float32) * scale_h, 'w_gate': jax.random.normal(ks[2], (E, I, H), dtype=jnp.float32) * scale_h, 'w_up': jax.random.normal(ks[3], (E, I, H), dtype=jnp.float32) * scale_h, 'w_down': jax.random.normal(ks[4], (E, H, I), dtype=jnp.float32) * scale_i}
    _L0_ffn_in = _L0_ffn_setup()
    _d = {'L0_attn_x': _L0_attn_in['x'], 'L0_attn_w_q': _L0_attn_in['w_q'], 'L0_attn_b_q': _L0_attn_in['b_q'], 'L0_attn_w_k': _L0_attn_in['w_k'], 'L0_attn_b_k': _L0_attn_in['b_k'], 'L0_attn_w_v': _L0_attn_in['w_v'], 'L0_attn_b_v': _L0_attn_in['b_v'], 'L0_attn_w_out': _L0_attn_in['w_out'], 'L0_attn_b_out': _L0_attn_in['b_out'], 'L0_ffn_gate_w': _L0_ffn_in['gate_w'], 'L0_ffn_w_gate': _L0_ffn_in['w_gate'], 'L0_ffn_w_up': _L0_ffn_in['w_up'], 'L0_ffn_w_down': _L0_ffn_in['w_down']}
    _x0 = _d['L0_attn_x']
    _d['L0_attn_x'] = jax.random.normal(jax.random.fold_in(jax.random.key(seed), 1), (8, 256, 128), dtype=_x0.dtype)
    del _x0
    return _d

def reference(L0_attn_x, L0_attn_w_q, L0_attn_b_q, L0_attn_w_k, L0_attn_b_k, L0_attn_w_v, L0_attn_b_v, L0_attn_w_out, L0_attn_b_out, L0_ffn_gate_w, L0_ffn_w_gate, L0_ffn_w_up, L0_ffn_w_down):

    def _L0_attn_ref(x, w_q, b_q, w_k, b_k, w_v, b_v, w_out, b_out):
        import jax, jax.numpy as jnp
        import numpy as np
        EMBED_DIM = 128
        D = x.shape[-1]
        scaling = 1.0 / jnp.sqrt(jnp.asarray(D, x.dtype))
        q = jnp.einsum('bsd,ed->bse', x, w_q) + b_q
        k = jnp.einsum('bsd,ed->bse', x, w_k) + b_k
        v = jnp.einsum('bsd,ed->bse', x, w_v) + b_v
        scores = jnp.einsum('bqd,bkd->bqk', q, k) * scaling
        attn = jax.nn.softmax(scores, axis=-1)
        out = jnp.einsum('bqk,bkd->bqd', attn, v)
        return jnp.einsum('bsd,ed->bse', out, w_out) + b_out

    def _L0_ffn_ref(hidden_states, gate_w, w_gate, w_up, w_down):
        import jax, jax.numpy as jnp
        import numpy as np
        B, S, H, I, E = (2, 512, 128, 64, 8)
        b, s, h = hidden_states.shape
        x = hidden_states.reshape(-1, h)
        logits = x @ gate_w.T
        top_v = jnp.max(logits, axis=-1)
        sel = jnp.argmax(logits, axis=-1)
        rw = jax.nn.sigmoid(top_v)
        out = jnp.zeros_like(x)
        n_exp = gate_w.shape[0]
        for e in range(n_exp):
            mask = (sel == e).astype(x.dtype)
            xs = x * (rw * mask)[:, None]
            g = xs @ w_gate[e].T
            u = xs @ w_up[e].T
            out = out + u * jax.nn.silu(g) @ w_down[e].T
        return out.reshape(b, s, h)
    x = L0_attn_x
    x = x + _L0_attn_ref(_layernorm(x, axis=-1), L0_attn_w_q, L0_attn_b_q, L0_attn_w_k, L0_attn_b_k, L0_attn_w_v, L0_attn_b_v, L0_attn_w_out, L0_attn_b_out)
    x = x + _L0_ffn_ref(_layernorm(x, axis=-1), L0_ffn_gate_w, L0_ffn_w_gate, L0_ffn_w_up, L0_ffn_w_down)
    return x

_drawn_inputs = setup_inputs


def setup_inputs(seed=0):
    import zlib

    import numpy as np

    out = dict(_drawn_inputs(seed))
    spreads = {}
    factors = {'L0_attn_b_q': 4.869, 'L0_attn_b_k': 8.0}
    for name, (base, spread) in spreads.items():
        noise = np.random.default_rng([zlib.crc32(name.encode()), seed]).standard_normal(out[name].shape)
        drawn = base * np.exp(spread * noise) if base else spread * noise
        out[name] = jnp.asarray(drawn.astype(out[name].dtype))
    for name, factor in factors.items():
        out[name] = (out[name] * factor).astype(out[name].dtype)
    return out
```

```python
from contextlib import ExitStack

import concourse.bass as bass
from concourse import mybir

F32 = mybir.dt.float32
F32R = mybir.dt.float32r
BF16 = mybir.dt.bfloat16
ALU = mybir.AluOpType
ACT = mybir.ActivationFunctionType
AX_X = mybir.AxisListType.X

P = 128
D = 128
BATCHES, SEQ = 8, 256
EXPERTS, HIDDEN = 8, 64
TILES = BATCHES * SEQ // P
BT = SEQ // P
GT = 4
GB = GT // BT
GROUPS = TILES // GT
GTOK = GT * P
CHUNKS = EXPERTS * HIDDEN // P
PER_CHUNK = P // HIDDEN
SCALE = float(D) ** -0.5
EPS = 1e-5
PENALTY = -1e30

WQ, WK, WV, WOT, BQ, BK, BV = 0, D, 2 * D, 3 * D, 4 * D, 4 * D + 1, 4 * D + 2
ATTN_COLS = 4 * D + 3


def layer_kernel(nc, x, attn_w, bo, gate_up_t, down_t, router_t, out):
    with ExitStack() as ctx:
        def sb(name, shape, dt=F32):
            return ctx.enter_context(nc.sbuf_tensor(name, shape, dt))

        def bank(name):
            return ctx.enter_context(nc.psum_tensor(name, [P, 512], F32))

        def sem(name):
            return ctx.enter_context(nc.semaphore(name))

        x_all = sb("x_all", [P, TILES, D])
        x_bias = sb("x_bias", [P, TILES, D])
        x_mid = sb("x_mid", [P, TILES, D])
        y_all = sb("y_all", [P, TILES, D])
        attn_sb = sb("attn_sb", [P, ATTN_COLS])
        bo_row = sb("bo_row", [1, D])
        gate_up = sb("gate_up", [P, 2, CHUNKS, P])
        gate_up_hi = sb("gate_up_hi", [P, 2, CHUNKS, P], F32R)
        gate_up_lo = sb("gate_up_lo", [P, 2, CHUNKS, P], F32R)
        down_w = sb("down_w", [P, CHUNKS, D])
        router_w = sb("router_w", [P, EXPERTS])
        ident = sb("ident", [P, P])
        ones = sb("ones", [P, P])
        bv_wide = sb("bv_wide", [P, P])
        bq_wide = sb("bq_wide", [P, P])
        prefer = sb("prefer", [P, GT, EXPERTS])
        penalty = sb("penalty", [EXPERTS, CHUNKS, PER_CHUNK, HIDDEN], BF16)
        scratch = sb("scratch", [1, 1])
        eps = sb("eps", [P, GT])
        half_neg = sb("half_neg", [P, TILES])
        m_sb = sb("m_sb", [P, D])
        q_bias = sb("q_bias", [P, 1])
        vo_sb = sb("vo_sb", [P, D + 1])
        out_bias = sb("out_bias", [P, D])
        qk_bias = sb("qk_bias", [P, 1])

        stats1 = sb("stats1", [P, TILES, 6])
        mv1 = sb("mv1", [P, TILES, 2])
        rstd1 = sb("rstd1", [P, TILES])
        xn = sb("xn", [P, GT, D])
        xn_t = sb("xn_t", [P, GTOK])
        q_t = sb("q_t", [P, GTOK])
        vo = sb("vo", [P, GT, D + 1])
        shift = sb("shift", [P, GT])
        neg_max = sb("neg_max", [P, GT])
        exp_bias = sb("exp_bias", [P, GT])
        probs = sb("probs", [P, GT, SEQ])
        row_sum = sb("row_sum", [P, GT])
        row_inv = sb("row_inv", [P, GT])
        probs_t = sb("probs_t", [P, GB, BT, SEQ])
        stats2 = sb("stats2", [P, GT, 6])
        mv2 = sb("mv2", [P, GT, 2])
        rstd2 = sb("rstd2", [P, GT])
        xm = sb("xm", [P, GT, D])
        xm_t = sb("xm_t", [P, GTOK])
        top = sb("top", [P, GT])
        is_top = sb("is_top", [P, GT, EXPERTS])
        first = sb("first", [P, GT])
        unrouted = sb("unrouted", [P, GT, EXPERTS])
        exp_top = sb("exp_top", [P, GT])
        exp_top1 = sb("exp_top1", [P, GT])
        route_w = sb("route_w", [P, GT])
        xs = sb("xs", [P, GT, D])
        xs_hi = sb("xs_hi", [P, GTOK], F32R)
        xs_lo = sb("xs_lo", [P, GTOK], F32R)
        unrouted_t = sb("unrouted_t", [EXPERTS, GTOK], BF16)
        tanh_g = sb("tanh_g", [P, 2, GTOK])
        silu2 = sb("silu2", [P, 2, GTOK])
        hid_t = sb("hid_t", [P, CHUNKS, GTOK])

        turn_bank = bank("turn_bank")
        qv_bank = bank("qv_bank")
        score_bank = bank("score_bank")
        probs_bank = bank("probs_bank")
        attn_bank = bank("attn_bank")
        gate_bank = bank("gate_bank")
        up_bank = bank("up_bank")
        down_bank = bank("down_bank")

        x_first_in, x_rest_in = sem("x_first_in"), sem("x_rest_in")
        attn_in, bo_in, gate_up_in, down_in, router_in = (
            sem("attn_in"), sem("bo_in"), sem("gate_up_in"), sem("down_in"), sem("router_in"))
        out_stored = sem("out_stored")
        ones_set, wide_set, half_set = sem("ones_set"), sem("wide_set"), sem("half_set")
        ident_set, penalty_set, prefer_set = sem("ident_set"), sem("penalty_set"), sem("prefer_set")
        weights_multiplied, weights_ready = sem("weights_multiplied"), sem("weights_ready")
        split_hi, split_ready = sem("split_hi"), sem("split_ready")
        x_bias_ready = sem("x_bias_ready")
        stats1_done, mv1_done, var1_done, rstd1_done, xn_done = (
            sem("stats1_done"), sem("mv1_done"), sem("var1_done"), sem("rstd1_done"), sem("xn_done"))
        xn_turned, xn_t_ready = sem("xn_turned"), sem("xn_t_ready")
        q_multiplied, q_ready = sem("q_multiplied"), sem("q_ready")
        vo_multiplied, vo_ready = sem("vo_multiplied"), sem("vo_ready")
        scored, max_done, bias_done, exp_done = (
            sem("scored"), sem("max_done"), sem("bias_done"), sem("exp_done"))
        shift_done, inv_done = sem("shift_done"), sem("inv_done")
        probs_turned, probs_t_ready = sem("probs_turned"), sem("probs_t_ready")
        attended, x_mid_done = sem("attended"), sem("x_mid_done")
        stats2_done, mv2_done, var2_done, rstd2_done, xm_done = (
            sem("stats2_done"), sem("mv2_done"), sem("var2_done"), sem("rstd2_done"), sem("xm_done"))
        xm_turned, xm_t_ready = sem("xm_turned"), sem("xm_t_ready")
        logits_done, top_done, top_exp_done = sem("logits_done"), sem("top_done"), sem("top_exp_done")
        weight_inv_done = sem("weight_inv_done")
        route_step = sem("route_step")
        unrouted_done, unrouted_turned, unrouted_t_ready = (
            sem("unrouted_done"), sem("unrouted_turned"), sem("unrouted_t_ready"))
        xs_done, xs_turned, xs_hi_ready, xs_lo_ready = (
            sem("xs_done"), sem("xs_turned"), sem("xs_hi_ready"), sem("xs_lo_ready"))
        gate_done, tanh_done, silu_done = sem("gate_done"), sem("tanh_done"), sem("silu_done")
        up_done, hid_done = sem("up_done"), sem("hid_done")
        down_done, y_done = sem("down_done"), sem("y_done")

        x_dram = x.rearrange("b (h p) d -> p (b h) d", p=P)
        out_dram = out.rearrange("b (h p) d -> p (b h) d", p=P)

        def group_tiles(buffer, g):
            return buffer[:, bass.ds(g * GT, GT), :]

        def tile_of(buffer, g, t):
            return buffer[:, bass.ds(g * GT + t, 1), :].rearrange("p a d -> p (a d)")

        def turned(t):
            return slice(t * P, (t + 1) * P)

        block = ctx.enter_context(nc.Block())

        @block.sync
        def _(sp):
            sp.dma_start(x_all[:, 0:GT, :], x_dram[:, 0:GT, :]).then_inc(x_first_in, 16)
            sp.dma_start(x_all[:, GT:TILES, :], x_dram[:, GT:TILES, :]).then_inc(x_rest_in, 16)
            sp.dma_start(down_w[:, :, :], down_t.rearrange("(c p) d -> p c d", p=P)).then_inc(down_in, 16)
            with sp.Fori(0, GROUPS) as h:
                sp.wait_ge(y_done, h + 1)
                sp.dma_start(group_tiles(out_dram, h), group_tiles(y_all, h)).then_inc(out_stored, 16)
            sp.wait_ge(out_stored, 16 * GROUPS)

        @block.gpsimd
        def _(pool):
            nc.gpsimd.memset(ident[:, :], 0.0).then_inc(ident_set, 1)
            pool.wait_ge(ident_set, 1)
            nc.gpsimd.affine_select(out=ident[:, :], in_=ident[:, :], compare_op=ALU.not_equal, fill=1.0,
                                    base=0, pattern=[[-1, P]], channel_multiplier=1).then_inc(ident_set, 1)

            def inverse_std1(first, last, step):
                pool.wait_ge(mv1_done, last)
                nc.gpsimd.tensor_scalar(rstd1[:, first:last], mv1[:, first:last, 1], EPS, None, ALU.add
                                        ).then_inc(var1_done, 1)
                pool.wait_ge(var1_done, step)
                nc.gpsimd.tensor_tensor(rstd1[:, first:last], rstd1[:, first:last], half_neg[:, first:last],
                                        ALU.pow).then_inc(rstd1_done, 1)

            def inverse_std2(g):
                pool.wait_ge(mv2_done, GT * g + GT)
                nc.gpsimd.tensor_tensor(rstd2[:, :], mv2[:, :, 1], eps[:, :], ALU.add).then_inc(var2_done, 1)
                pool.wait_ge(var2_done, g + 1)
                nc.gpsimd.tensor_tensor(rstd2[:, :], rstd2[:, :], half_neg[:, 0:GT], ALU.pow
                                        ).then_inc(rstd2_done, 1)

            def add_bias(g):
                nc.gpsimd.tensor_tensor(group_tiles(x_bias, g), group_tiles(x_all, g),
                                        out_bias[:, :].rearrange("p (a d) -> p a d", a=1).broadcast_to([P, GT, D]),
                                        ALU.add).then_inc(x_bias_ready, 1)

            pool.wait_ge(half_set, 2)
            inverse_std1(0, GT, 1)
            nc.gpsimd.memset(penalty[:, :, :, :], 0.0).then_inc(penalty_set, 1)
            pool.wait_ge(penalty_set, 1)
            nc.gpsimd.affine_select(out=penalty[:, :, :, :], in_=penalty[:, :, :, :], compare_op=ALU.not_equal,
                                    fill=PENALTY, base=0,
                                    pattern=[[-PER_CHUNK, CHUNKS], [-1, PER_CHUNK], [0, HIDDEN]],
                                    channel_multiplier=1).then_inc(penalty_set, 1)
            nc.gpsimd.iota(prefer[:, :, :], pattern=[[0, GT], [-1, EXPERTS]], base=EXPERTS,
                           channel_multiplier=0, allow_small_or_imprecise_dtypes=True).then_inc(prefer_set, 1)
            pool.wait_ge(weights_ready, 1)
            add_bias(0)
            pool.wait_ge(gate_up_in, 16)
            nc.gpsimd.tensor_copy(gate_up_hi[:, :, :, :], gate_up[:, :, :, :]).then_inc(split_hi, 1)
            pool.wait_ge(split_hi, 1)
            nc.gpsimd.tensor_tensor(gate_up_lo[:, :, :, :], gate_up[:, :, :, :],
                                    gate_up_hi[:, :, :, :].bitcast(F32), ALU.subtract).then_inc(split_ready, 1)
            inverse_std1(GT, TILES, 2)
            inverse_std2(0)
            pool.wait_ge(x_rest_in, 16)
            with pool.Fori(1, GROUPS) as g:
                add_bias(g)
                inverse_std2(g)

        @block.scalar
        def _(act):
            act.dma_start(attn_sb[:, :], attn_w).then_inc(attn_in, 16)
            act.dma_start(bo_row[:, :], bo).then_inc(bo_in, 16)
            act.dma_start(gate_up[:, :, :, :], gate_up_t.rearrange("d (a c p) -> d a c p", a=2, p=P)
                          ).then_inc(gate_up_in, 16)
            act.dma_start(router_w[:, :], router_t).then_inc(router_in, 16)
            nc.scalar.preload_act_table(ACT.Exp)

            def weight_products():
                act.wait_ge(weights_multiplied, 1)
                nc.scalar.activation(m_sb[:, :], gate_bank[:, 0:D], ACT.Copy)
                nc.scalar.activation(q_bias[:, :], gate_bank[:, D:D + 1], ACT.Copy, scale=SCALE)
                nc.scalar.activation(vo_sb[:, 0:D], gate_bank[:, 2 * D:3 * D], ACT.Copy)
                nc.scalar.activation(vo_sb[:, D:D + 1], gate_bank[:, 3 * D:3 * D + 1], ACT.Copy, scale=SCALE)
                nc.scalar.activation(qk_bias[:, :], up_bank[:, D:D + 1], ACT.Copy, scale=SCALE)
                nc.scalar.activation(out_bias[:, :], up_bank[:, 0:D], ACT.Copy).then_inc(weights_ready, 1)

            def keep_xn(g):
                act.wait_ge(xn_turned, g + 1)
                nc.scalar.activation(xn_t[:, :], turn_bank[:, :], ACT.Copy).then_inc(xn_t_ready, 1)

            def keep_q(g):
                act.wait_ge(q_multiplied, g + 1)
                nc.scalar.activation(q_t[:, :], qv_bank[:, :], ACT.Identity, scale=SCALE,
                                     bias=q_bias[:, 0:1]).then_inc(q_ready, 1)

            def keep_vo(g, b):
                source = (probs_bank, qv_bank)[b]
                act.wait_ge(vo_multiplied, GB * g + b + 1)
                nc.scalar.activation(vo[:, BT * b:BT * b + BT, :],
                                     source[:, 0:BT * (D + 1)].rearrange("p (t n) -> p t n", t=BT),
                                     ACT.Copy).then_inc(vo_ready, 1)

            def exponents(g, b):
                act.wait_ge(bias_done, GT * g + BT * b + BT)
                for t in range(BT * b, BT * b + BT):
                    nc.scalar.activation(probs[:, t, :], score_bank[:, (t % BT) * SEQ:(t % BT + 1) * SEQ], ACT.Exp,
                                         bias=exp_bias[:, t:t + 1],
                                         accum_out=row_sum[:, t:t + 1]).then_inc(exp_done, 1)

            def keep_probs(g, b):
                act.wait_ge(probs_turned, GB * g + b + 1)
                nc.scalar.activation(probs_t[:, b, :, :], probs_bank[:, :].rearrange("p (j i) -> p j i", j=BT),
                                     ACT.Copy).then_inc(probs_t_ready, 1)

            def keep_xm(g):
                act.wait_ge(xm_turned, g + 1)
                nc.scalar.activation(xm_t[:, :], turn_bank[:, :], ACT.Copy).then_inc(xm_t_ready, 1)

            def exp_of_top(g):
                act.wait_ge(top_done, g + 1)
                nc.scalar.activation(exp_top[:, :], top[:, :], ACT.Exp, scale=-1.0).then_inc(top_exp_done, 1)

            def keep_unrouted(g):
                act.wait_ge(unrouted_turned, g + 1)
                nc.scalar.activation(unrouted_t[:, :], attn_bank[0:EXPERTS, :], ACT.Copy
                                     ).then_inc(unrouted_t_ready, 1)

            def round_xs(g):
                act.wait_ge(xs_turned, g + 1)
                nc.scalar.activation(xs_hi[:, :], turn_bank[:, :], ACT.Copy).then_inc(xs_hi_ready, 1)

            def tanh_of_gate(h, c):
                act.wait_ge(gate_done, CHUNKS * h + c + 1)
                if c >= 2:
                    act.wait_ge(silu_done, CHUNKS * h + c - 1)
                nc.scalar.activation(tanh_g[:, c % 2, :], gate_bank[:, :], ACT.Tanh, scale=0.5
                                     ).then_inc(tanh_done, 1)

            weight_products()
            keep_xn(0)
            keep_q(0)
            keep_vo(0, 0)
            keep_vo(0, 1)
            exponents(0, 0)
            exponents(0, 1)
            keep_probs(0, 0)
            keep_probs(0, 1)
            keep_xm(0)
            exp_of_top(0)
            keep_unrouted(0)
            round_xs(0)
            with act.Fori(1, GROUPS) as g:
                h = g - 1
                keep_xn(g)
                tanh_of_gate(h, 0)
                keep_q(g)
                keep_vo(g, 0)
                keep_vo(g, 1)
                exponents(g, 0)
                tanh_of_gate(h, 1)
                keep_probs(g, 0)
                exponents(g, 1)
                tanh_of_gate(h, 2)
                keep_probs(g, 1)
                tanh_of_gate(h, 3)
                keep_xm(g)
                exp_of_top(g)
                keep_unrouted(g)
                round_xs(g)
            for c in range(CHUNKS):
                tanh_of_gate(GROUPS - 1, c)

        @block.vector
        def _(dve):
            nc.vector.memset(eps[:, :], EPS).then_inc(half_set, 1)
            nc.vector.memset(half_neg[:, :], -0.5).then_inc(half_set, 1)
            nc.vector.memset(ones[:, :], 1.0).then_inc(ones_set, 1)

            def statistics1(first, last):
                for t in range(first, last):
                    nc.vector.bn_stats(stats1[:, t, :], x_all[:, t, :]).then_inc(stats1_done, 1)
                for t in range(first, last):
                    dve.wait_ge(stats1_done, t + 1)
                    nc.vector.bn_aggr(mv1[:, t, :], stats1[:, t, :]).then_inc(mv1_done, 1)

            def normalise1(g):
                for t in range(GT):
                    i = g * GT + t
                    nc.vector.tensor_scalar(xn[:, t, :], tile_of(x_all, g, t),
                                            mv1[:, bass.ds(i, 1), 0:1].rearrange("p a b -> p (a b)"),
                                            rstd1[:, bass.ds(i, 1)],
                                            ALU.subtract, ALU.mult).then_inc(xn_done, 1)

            def carry_wait():
                nc.vector.memset(scratch[:, :], 0.0)

            def statistics2(g):
                dve.wait_ge(x_mid_done, GT * g + GT)
                carry_wait()
                for t in range(GT):
                    nc.vector.bn_stats(stats2[:, t, :], tile_of(x_mid, g, t)).then_inc(stats2_done, 1)
                dve.wait_ge(stats2_done, GT * g + GT)
                carry_wait()
                for t in range(GT):
                    nc.vector.bn_aggr(mv2[:, t, :], stats2[:, t, :]).then_inc(mv2_done, 1)

            def normalise2(g):
                dve.wait_ge(rstd2_done, g + 1)
                for t in range(GT):
                    nc.vector.tensor_scalar(xm[:, t, :], tile_of(x_mid, g, t), mv2[:, t, 0:1],
                                            rstd2[:, t:t + 1], ALU.subtract, ALU.mult).then_inc(xm_done, 1)

            def row_shift(g):
                dve.wait_ge(vo_ready, GB * g + GB)
                nc.vector.tensor_scalar(shift[:, :], vo[:, :, D], qk_bias[:, 0:1], None, ALU.add
                                        ).then_inc(shift_done, 1)

            def row_maxima(g, b):
                tiles = slice(BT * b, BT * b + BT)
                dve.wait_ge(scored, GB * g + b + 1)
                nc.vector.tensor_reduce(neg_max[:, tiles], score_bank[:, :].rearrange("p (t j) -> p t j", t=BT),
                                        AX_X, ALU.max, negate=True).then_inc(max_done, 1)
                dve.wait_ge(shift_done, g + 1)
                dve.wait_ge(max_done, GB * g + b + 1)
                for t in range(BT * b, BT * b + BT):
                    nc.vector.tensor_scalar(exp_bias[:, t:t + 1], neg_max[:, t:t + 1], shift[:, t:t + 1],
                                            shift[:, t:t + 1], ALU.subtract, ALU.add).then_inc(bias_done, 1)

            def add_attention(g, b):
                tiles = slice(BT * b, BT * b + BT)
                dve.wait_ge(exp_done, GT * g + BT * b + BT)
                nc.vector.reciprocal(row_inv[:, tiles], row_sum[:, tiles]).then_inc(inv_done, 1)
                dve.wait_ge(x_bias_ready, g + 1)
                dve.wait_ge(inv_done, GB * g + b + 1)
                dve.wait_ge(attended, GB * g + b + 1)
                for t in range(BT * b, BT * b + BT):
                    nc.vector.scalar_tensor_tensor(
                        out=tile_of(x_mid, g, t), in0=attn_bank[:, (t % BT) * D:(t % BT + 1) * D],
                        scalar=row_inv[:, t:t + 1], in1=tile_of(x_bias, g, t), op0=ALU.mult, op1=ALU.add
                    ).then_inc(x_mid_done, 1)

            ROUTE_STEPS = 4

            def route(g):
                logits = attn_bank[:, 0:GT * EXPERTS].rearrange("p (t e) -> p t e", t=GT)

                def spread(v):
                    return v[:, :].rearrange("p (t a) -> p t a", a=1).broadcast_to([P, GT, EXPERTS])

                def own_step(k):
                    dve.wait_ge(route_step, ROUTE_STEPS * g + k)
                dve.wait_ge(logits_done, g + 1)
                nc.vector.tensor_reduce(top[:, :], logits, AX_X, ALU.max).then_inc(top_done, 1)
                dve.wait_ge(top_done, g + 1)
                nc.vector.tensor_tensor(is_top[:, :, :], logits, spread(top), ALU.is_equal).then_inc(route_step, 1)
                own_step(1)
                nc.vector.tensor_tensor(is_top[:, :, :], is_top[:, :, :], prefer[:, :, :], ALU.mult
                                        ).then_inc(route_step, 1)
                own_step(2)
                nc.vector.tensor_reduce(first[:, :], is_top[:, :, :], AX_X, ALU.max).then_inc(route_step, 1)
                dve.wait_ge(top_exp_done, g + 1)
                nc.vector.tensor_scalar(exp_top1[:, :], exp_top[:, :], 1.0, None, ALU.add).then_inc(route_step, 1)
                own_step(3)
                nc.vector.tensor_tensor(unrouted[:, :, :], is_top[:, :, :], spread(first), ALU.not_equal
                                        ).then_inc(unrouted_done, 1)
                own_step(4)
                nc.vector.reciprocal(route_w[:, :], exp_top1[:, :]).then_inc(weight_inv_done, 1)
                dve.wait_ge(weight_inv_done, g + 1)
                for t in range(GT):
                    nc.vector.tensor_scalar(xs[:, t, :], xm[:, t, :], route_w[:, t:t + 1], None, ALU.mult
                                            ).then_inc(xs_done, 1)

            def rest_of_xs(g):
                dve.wait_ge(xs_hi_ready, g + 1)
                nc.vector.tensor_tensor(xs_lo[:, :], turn_bank[:, :], xs_hi[:, :].bitcast(F32), ALU.subtract
                                        ).then_inc(xs_lo_ready, 1)

            def silu_of_gate(h, c):
                dve.wait_ge(tanh_done, CHUNKS * h + c + 1)
                nc.vector.scalar_tensor_tensor(out=silu2[:, c % 2, :], in0=tanh_g[:, c % 2, :], scalar=1.0,
                                               in1=gate_bank[:, :], op0=ALU.add, op1=ALU.mult
                                               ).then_inc(silu_done, 1)

            def hidden(h, c):
                dve.wait_ge(up_done, CHUNKS * h + c + 1)
                dve.wait_ge(silu_done, CHUNKS * h + c + 1)
                nc.vector.scalar_tensor_tensor(out=hid_t[:, c, :], in0=up_bank[:, :], scalar=0.5,
                                               in1=silu2[:, c % 2, :], op0=ALU.mult, op1=ALU.mult
                                               ).then_inc(hid_done, 1)

            def add_experts(h):
                dve.wait_ge(down_done, h + 1)
                nc.vector.tensor_tensor(group_tiles(y_all, h),
                                        down_bank[:, :].rearrange("p (t d) -> p t d", t=GT),
                                        group_tiles(x_mid, h), ALU.add).then_inc(y_done, 1)

            dve.wait_ge(x_first_in, 16)
            statistics1(0, GT)
            dve.wait_ge(attn_in, 16)
            nc.vector.tensor_copy(bv_wide[:, :], attn_sb[:, BV:BV + 1].broadcast_to([P, P])).then_inc(wide_set, 1)
            nc.vector.tensor_copy(bq_wide[:, :], attn_sb[:, BQ:BQ + 1].broadcast_to([P, P])).then_inc(wide_set, 1)
            dve.wait_ge(rstd1_done, 1)
            normalise1(0)
            dve.wait_ge(x_rest_in, 16)
            statistics1(GT, TILES)
            dve.wait_ge(weights_ready, 1)
            row_shift(0)
            row_maxima(0, 0)
            row_maxima(0, 1)
            add_attention(0, 0)
            add_attention(0, 1)
            statistics2(0)
            normalise2(0)
            dve.wait_ge(prefer_set, 1)
            route(0)
            rest_of_xs(0)
            dve.wait_ge(rstd1_done, 2)
            with dve.Fori(1, GROUPS) as g:
                h = g - 1
                dve.wait_ge(xn_turned, g)
                normalise1(g)
                silu_of_gate(h, 0)
                hidden(h, 0)
                row_shift(g)
                row_maxima(g, 0)
                silu_of_gate(h, 1)
                hidden(h, 1)
                row_maxima(g, 1)
                add_attention(g, 0)
                silu_of_gate(h, 2)
                hidden(h, 2)
                add_attention(g, 1)
                statistics2(g)
                silu_of_gate(h, 3)
                hidden(h, 3)
                normalise2(g)
                add_experts(h)
                route(g)
                rest_of_xs(g)
            for c in range(CHUNKS):
                silu_of_gate(GROUPS - 1, c)
                hidden(GROUPS - 1, c)
            add_experts(GROUPS - 1)

        @block.tensor
        def _(pe):
            def weight_products():
                wq, wk, wv, wo_t = (attn_sb[:, w:w + D] for w in (WQ, WK, WV, WOT))
                pe.wait_ge(attn_in, 16)
                nc.tensor.matmul(gate_bank[:, 0:D], wq, wk, start=True, stop=True)
                nc.tensor.matmul(gate_bank[:, D:D + 1], wk, attn_sb[:, BQ:BQ + 1], start=True, stop=True)
                nc.tensor.matmul(gate_bank[:, 2 * D:3 * D], wv, wo_t, start=True, stop=True)
                nc.tensor.matmul(gate_bank[:, 3 * D:3 * D + 1], wq, attn_sb[:, BK:BK + 1], start=True, stop=True)
                pe.wait_ge(wide_set, 2)
                nc.tensor.matmul(up_bank[:, D:D + 1], bq_wide[:, :], attn_sb[:, BK:BK + 1], start=True, stop=True)
                pe.wait_ge(ones_set, 1)
                pe.wait_ge(bo_in, 16)
                nc.tensor.matmul(up_bank[:, 0:D], bv_wide[:, :], wo_t, start=True, stop=False)
                nc.tensor.matmul(up_bank[:, 0:D], ones[0:1, :], bo_row[:, :], start=False, stop=True
                                 ).then_inc(weights_multiplied, 1)

            def turn(source, done):
                for t in range(GT):
                    last = nc.tensor.transpose(turn_bank[:, turned(t)], source[:, t, :], ident[:, :])
                last.then_inc(done, 1)

            def turn_xn(g, first=False):
                pe.wait_ge(xn_done, GT * g + GT)
                if not first:
                    pe.wait_ge(xs_lo_ready, g)
                turn(xn, xn_turned)

            def query(g):
                pe.wait_ge(xn_t_ready, g + 1)
                nc.tensor.matmul(qv_bank[:, :], m_sb[:, :], xn_t[:, :], start=True, stop=True
                                 ).then_inc(q_multiplied, 1)

            def value(g, b):
                if b == 1:
                    pe.wait_ge(q_ready, g + 1)
                target = (probs_bank, qv_bank)[b]
                for t in range(BT):
                    last = nc.tensor.matmul(target[:, t * (D + 1):(t + 1) * (D + 1)], xn_t[:, turned(BT * b + t)],
                                            vo_sb[:, :], start=True, stop=True)
                last.then_inc(vo_multiplied, 1)

            def scores(g, b):
                pe.wait_ge(q_ready, g + 1)
                if b == 1:
                    pe.wait_ge(exp_done, GT * g + BT)
                for t in range(BT):
                    last = nc.tensor.matmul(score_bank[:, t * SEQ:(t + 1) * SEQ], q_t[:, turned(BT * b + t)],
                                            xn_t[:, b * SEQ:(b + 1) * SEQ], start=True, stop=True)
                last.then_inc(scored, 1)

            def turn_probs(g, b):
                pe.wait_ge(exp_done, GT * g + BT * b + BT)
                if b == 0:
                    pe.wait_ge(vo_ready, GB * g + 1)
                else:
                    pe.wait_ge(probs_t_ready, GB * g + 1)
                for j in range(BT):
                    for t in range(BT):
                        last = nc.tensor.transpose(probs_bank[:, j * SEQ + t * P:j * SEQ + (t + 1) * P],
                                                   probs[:, BT * b + t, j * P:(j + 1) * P], ident[:, :])
                last.then_inc(probs_turned, 1)

            def attend(g, b):
                pe.wait_ge(probs_t_ready, GB * g + b + 1)
                pe.wait_ge(vo_ready, GB * g + b + 1)
                if b == 1:
                    pe.wait_ge(x_mid_done, GT * g + BT)
                for t in range(BT):
                    for j in range(BT):
                        last = nc.tensor.matmul(attn_bank[:, t * D:(t + 1) * D],
                                                probs_t[:, b, j, t * P:(t + 1) * P], vo[:, BT * b + j, 0:D],
                                                start=(j == 0), stop=(j == BT - 1))
                last.then_inc(attended, 1)

            def turn_xm(g):
                pe.wait_ge(xm_done, GT * g + GT)
                turn(xm, xm_turned)

            def logits(g):
                pe.wait_ge(xm_t_ready, g + 1)
                for t in range(GT):
                    last = nc.tensor.matmul(attn_bank[:, t * EXPERTS:(t + 1) * EXPERTS], xm_t[:, turned(t)],
                                            router_w[:, :], start=True, stop=True)
                last.then_inc(logits_done, 1)

            def turn_unrouted(g):
                pe.wait_ge(unrouted_done, g + 1)
                for t in range(GT):
                    last = nc.tensor.transpose(attn_bank[0:EXPERTS, turned(t)], unrouted[:, t, :], ident[:, :])
                last.then_inc(unrouted_turned, 1)

            def turn_xs(g):
                pe.wait_ge(xs_done, GT * g + GT)
                turn(xs, xs_turned)

            def split_product(target, which, c, opened):
                w_hi, w_lo = gate_up_hi[:, which, c, :], gate_up_lo[:, which, c, :]
                nc.tensor.matmul(target, w_lo, xs_hi[:, :], start=not opened, stop=False)
                nc.tensor.matmul(target, w_hi, xs_lo[:, :], start=False, stop=False)
                return nc.tensor.matmul(target, w_hi, xs_hi[:, :], start=False, stop=True)

            def gate(h, c):
                if c == 0:
                    pe.wait_ge(xs_lo_ready, h + 1)
                    pe.wait_ge(unrouted_t_ready, h + 1)
                else:
                    pe.wait_ge(silu_done, CHUNKS * h + c)
                nc.tensor.matmul(gate_bank[:, :], penalty[:, c, :, :].rearrange("e s i -> e (s i)"),
                                 unrouted_t[:, :], start=True, stop=False)
                split_product(gate_bank[:, :], 0, c, True).then_inc(gate_done, 1)

            def up(h, c):
                if c > 0:
                    pe.wait_ge(hid_done, CHUNKS * h + c)
                split_product(up_bank[:, :], 1, c, False).then_inc(up_done, 1)

            def down(h, t):
                if t == 0:
                    pe.wait_ge(hid_done, CHUNKS * h + CHUNKS)
                for c in range(CHUNKS):
                    last = nc.tensor.matmul(down_bank[:, turned(t)], hid_t[:, c, turned(t)], down_w[:, c, :],
                                            start=(c == 0), stop=(c == CHUNKS - 1))
                if t == GT - 1:
                    last.then_inc(down_done, 1)

            weight_products()
            pe.wait_ge(ident_set, 2)
            turn_xn(0, first=True)
            pe.wait_ge(weights_ready, 1)
            query(0)
            value(0, 0)
            value(0, 1)
            scores(0, 0)
            scores(0, 1)
            turn_probs(0, 0)
            turn_probs(0, 1)
            attend(0, 0)
            attend(0, 1)
            turn_xm(0)
            pe.wait_ge(router_in, 16)
            logits(0)
            turn_xs(0)
            turn_unrouted(0)
            pe.wait_ge(split_ready, 1)
            pe.wait_ge(penalty_set, 2)
            pe.wait_ge(down_in, 16)
            with pe.Fori(1, GROUPS) as g:
                h = g - 1
                turn_xn(g)
                gate(h, 0)
                query(g)
                up(h, 0)
                value(g, 0)
                value(g, 1)
                scores(g, 0)
                gate(h, 1)
                scores(g, 1)
                up(h, 1)
                turn_probs(g, 0)
                gate(h, 2)
                turn_probs(g, 1)
                up(h, 2)
                attend(g, 0)
                gate(h, 3)
                attend(g, 1)
                up(h, 3)
                down(h, 0)
                down(h, 1)
                turn_xm(g)
                down(h, 2)
                logits(g)
                down(h, 3)
                turn_unrouted(g)
                turn_xs(g)
            for c in range(CHUNKS):
                gate(GROUPS - 1, c)
                up(GROUPS - 1, c)
            for t in range(GT):
                down(GROUPS - 1, t)


def kernel(**inputs):
    import numpy as np
    import concourse.bacc as bacc
    from concourse.bass_utils import run_bass_kernel_spmd

    def f32(name):
        return np.asarray(inputs[name])

    def column(name):
        return f32(name).reshape(D, 1)

    arrays = {
        "x": f32("L0_attn_x"),
        "attn_w": np.concatenate([f32("L0_attn_w_q"), f32("L0_attn_w_k"), f32("L0_attn_w_v"), f32("L0_attn_w_out").T,
                                  column("L0_attn_b_q"), column("L0_attn_b_k"), column("L0_attn_b_v")], axis=1),
        "bo": f32("L0_attn_b_out").reshape(1, D),
        "gate_up_t": np.concatenate([f32("L0_ffn_w_gate").reshape(EXPERTS * HIDDEN, D).T,
                                     f32("L0_ffn_w_up").reshape(EXPERTS * HIDDEN, D).T], axis=1),
        "down_t": f32("L0_ffn_w_down").transpose(0, 2, 1).reshape(EXPERTS * HIDDEN, D),
        "router_t": f32("L0_ffn_gate_w").T,
    }
    nc = bacc.Bacc("TRN2", target_bir_lowering=False, num_devices=1)
    sent, args = {}, []
    for name, a in arrays.items():
        a = np.ascontiguousarray(a)
        sent[f"in_{name}"] = a
        args.append(nc.dram_tensor(f"in_{name}", a.shape, mybir.dt.from_np(a.dtype), kind="ExternalInput").ap())
    out = nc.dram_tensor("out_x", [BATCHES, SEQ, D], F32, kind="ExternalOutput").ap()
    layer_kernel(nc, *args, out)
    result = run_bass_kernel_spmd(nc, [sent], core_ids=[0])
    return result.results[0]["out_x"]
```

```python
from contextlib import ExitStack

import concourse.bass as bass
from concourse import mybir

F32 = mybir.dt.float32
F32R = mybir.dt.float32r
BF16 = mybir.dt.bfloat16
ALU = mybir.AluOpType
ACT = mybir.ActivationFunctionType
AX_X = mybir.AxisListType.X

P = 128
D = 128
BATCHES, SEQ = 8, 256
EXPERTS, HIDDEN = 8, 64
BT = SEQ // P
TILES = BATCHES * BT
CHUNKS = EXPERTS * HIDDEN // P
PER_CHUNK = P // HIDDEN
SCALE = float(D) ** -0.5
EPS = 1e-5
PENALTY = -1e30
LOOPED = 2
PAIRS = (BATCHES - LOOPED) // 2

WQ, WK, WV, WOT, BQ, BK, BV = 0, D, 2 * D, 3 * D, 4 * D, 4 * D + 1, 4 * D + 2
ATTN_COLS = 4 * D + 3


def layer_kernel(nc, x, attn_w, bo, gate_up_t, down_t, router_t, out):
    with ExitStack() as ctx:
        def sb(name, shape, dt=F32):
            return ctx.enter_context(nc.sbuf_tensor(name, shape, dt))

        def bank(name):
            return ctx.enter_context(nc.psum_tensor(name, [P, 512], F32))

        def sem(name):
            return ctx.enter_context(nc.semaphore(name))

        x_all = sb("x_all", [P, TILES, D])
        x_bias = sb("x_bias", [P, TILES, D])
        x_mid = sb("x_mid", [P, TILES, D])
        y_all = sb("y_all", [P, TILES, D])
        attn_sb = sb("attn_sb", [P, ATTN_COLS])
        bo_row = sb("bo_row", [1, D])
        gate_up = sb("gate_up", [P, 2, CHUNKS, P])
        gate_up_hi = sb("gate_up_hi", [P, 2, CHUNKS, P], F32R)
        gate_up_lo = sb("gate_up_lo", [P, 2, CHUNKS, P], F32R)
        down_w = sb("down_w", [P, CHUNKS, D])
        router_w = sb("router_w", [P, EXPERTS])
        ident = sb("ident", [P, P])
        ones = sb("ones", [P, P])
        bv_wide = sb("bv_wide", [P, P])
        bq_wide = sb("bq_wide", [P, P])
        prefer = sb("prefer", [P, BT, EXPERTS])
        penalty = sb("penalty", [EXPERTS, CHUNKS, PER_CHUNK, HIDDEN], BF16)
        scratch = sb("scratch", [1, 1])
        eps = sb("eps", [P, TILES])
        half_neg = sb("half_neg", [P, TILES])
        m_sb = sb("m_sb", [P, D])
        q_bias = sb("q_bias", [P, 1])
        vo_sb = sb("vo_sb", [P, D + 1])
        out_bias = sb("out_bias", [P, D])
        qk_bias = sb("qk_bias", [P, 1])
        stats1 = sb("stats1", [P, TILES, 6])
        mv1 = sb("mv1", [P, TILES, 2])
        rstd1 = sb("rstd1", [P, TILES])
        shift1 = sb("shift1", [P, TILES])

        xn = sb("xn", [P, 2, BT, D])
        xn_t = sb("xn_t", [P, 2, SEQ])
        q_t = sb("q_t", [P, 2, SEQ])
        vo = sb("vo", [P, 2, BT, D + 1])
        shift = sb("shift", [P, 2, BT])
        neg_max = sb("neg_max", [P, 2, BT])
        neg_max_less = sb("neg_max_less", [P, 2, BT])
        exp_bias = sb("exp_bias", [P, 2, BT])
        probs = sb("probs", [P, 2, BT, SEQ])
        row_sum = sb("row_sum", [P, 2, BT])
        row_inv = sb("row_inv", [P, 2, BT])
        probs_t = sb("probs_t", [P, 2, BT, SEQ])
        stats2 = sb("stats2", [P, 2, BT, 6])
        mv2 = sb("mv2", [P, 2, BT, 2])
        var2 = sb("var2", [P, 2, BT])
        rstd2 = sb("rstd2", [P, 2, BT])
        xm = sb("xm", [P, 2, BT, D])
        xm_t = sb("xm_t", [P, 2, SEQ])
        top = sb("top", [P, 2, BT])
        is_top = sb("is_top", [P, 2, BT, EXPERTS])
        ranked = sb("ranked", [P, 2, BT, EXPERTS])
        first = sb("first", [P, 2, BT])
        unrouted = sb("unrouted", [P, 2, BT, EXPERTS])
        exp_top = sb("exp_top", [P, 2, BT])
        exp_top1 = sb("exp_top1", [P, 2, BT])
        route_w = sb("route_w", [P, 2, BT])
        xs = sb("xs", [P, 2, BT, D])
        xs_hi = sb("xs_hi", [P, 2, SEQ], F32R)
        xs_lo = sb("xs_lo", [P, 2, SEQ], F32R)
        unrouted_t = sb("unrouted_t", [EXPERTS, 2, SEQ], BF16)
        hid_t = sb("hid_t", [P, 2, CHUNKS, SEQ])
        tanh_g = sb("tanh_g", [P, 2, SEQ])
        silu2 = sb("silu2", [P, 2, SEQ])

        turn_bank = bank("turn_bank")
        query_bank = bank("query_bank")
        score_bank = bank("score_bank")
        probs_bank = bank("probs_bank")
        attn_bank = bank("attn_bank")
        gate_up_banks = (bank("gate_up_even"), bank("gate_up_odd"))
        down_bank = bank("down_bank")

        x_first_in, x_rest_in = sem("x_first_in"), sem("x_rest_in")
        attn_in, bo_in, gate_up_in, down_in, router_in = (
            sem("attn_in"), sem("bo_in"), sem("gate_up_in"), sem("down_in"), sem("router_in"))
        out_stored = sem("out_stored")
        filled, wide_set = sem("filled"), sem("wide_set")
        ident_set, penalty_set, prefer_set = sem("ident_set"), sem("penalty_set"), sem("prefer_set")
        weights_multiplied, weights_ready = sem("weights_multiplied"), sem("weights_ready")
        split_hi, split_ready = sem("split_hi"), sem("split_ready")
        stats1_done, mv1_done, var1_done, rstd1_done, shift1_done = (
            sem("stats1_done"), sem("mv1_done"), sem("var1_done"), sem("rstd1_done"), sem("shift1_done"))
        xn_done, xn_turned, xn_t_ready = sem("xn_done"), sem("xn_turned"), sem("xn_t_ready")
        q_multiplied, q_ready = sem("q_multiplied"), sem("q_ready")
        vo_multiplied, vo_ready = sem("vo_multiplied"), sem("vo_ready")
        scored, max_done, less_done, bias_done, exp_done = (
            sem("scored"), sem("max_done"), sem("less_done"), sem("bias_done"), sem("exp_done"))
        shift_done, row_inv_done, x_bias_ready = sem("shift_done"), sem("row_inv_done"), sem("x_bias_ready")
        probs_turned, probs_t_ready = sem("probs_turned"), sem("probs_t_ready")
        attended, x_mid_done = sem("attended"), sem("x_mid_done")
        stats2_done, mv2_done, var2_done, rstd2_done, xm_done = (
            sem("stats2_done"), sem("mv2_done"), sem("var2_done"), sem("rstd2_done"), sem("xm_done"))
        xm_turned, xm_t_ready = sem("xm_turned"), sem("xm_t_ready")
        logits_done, top_done, top_exp_done = sem("logits_done"), sem("top_done"), sem("top_exp_done")
        is_top_done, ranked_done, first_done, unrouted_done = (
            sem("is_top_done"), sem("ranked_done"), sem("first_done"), sem("unrouted_done"))
        exp_top1_done, route_w_done = sem("exp_top1_done"), sem("route_w_done")
        unrouted_turned, unrouted_t_ready = sem("unrouted_turned"), sem("unrouted_t_ready")
        xs_done, xs_turned, xs_hi_ready, xs_lo_ready = (
            sem("xs_done"), sem("xs_turned"), sem("xs_hi_ready"), sem("xs_lo_ready"))
        gate_up_done, tanh_done, silu_done, hid_done = (
            sem("gate_up_done"), sem("tanh_done"), sem("silu_done"), sem("hid_done"))
        down_done, y_done = sem("down_done"), sem("y_done")

        x_dram = x.rearrange("b (h p) d -> p (b h) d", p=P)
        out_dram = out.rearrange("b (h p) d -> p (b h) d", p=P)

        def batch_tiles(buffer, b):
            return buffer[:, bass.ds(b * BT, BT), :]

        def tile_of(buffer, b, t):
            return buffer[:, bass.ds(b * BT + t, 1), :].rearrange("p a d -> p (a d)")

        def cols(t, width=P):
            return slice(t * width, (t + 1) * width)

        block = ctx.enter_context(nc.Block())

        @block.sync
        def _(sp):
            sp.dma_start(x_all[:, 0:BT, :], x_dram[:, 0:BT, :]).then_inc(x_first_in, 16)
            sp.dma_start(x_all[:, BT:TILES, :], x_dram[:, BT:TILES, :]).then_inc(x_rest_in, 16)
            sp.dma_start(down_w[:, :, :], down_t.rearrange("(c p) d -> p c d", p=P)).then_inc(down_in, 16)
            with sp.Fori(0, BATCHES) as h:
                sp.wait_ge(y_done, h + 1)
                sp.dma_start(batch_tiles(out_dram, h), batch_tiles(y_all, h)).then_inc(out_stored, 16)
            sp.wait_ge(out_stored, 16 * BATCHES)

        @block.gpsimd
        def _(pool):
            nc.gpsimd.memset(ident[:, :], 0.0).then_inc(ident_set, 1)
            pool.wait_ge(ident_set, 1)
            nc.gpsimd.affine_select(out=ident[:, :], in_=ident[:, :], compare_op=ALU.not_equal, fill=1.0,
                                    base=0, pattern=[[-1, P]], channel_multiplier=1).then_inc(ident_set, 1)

            def inverse_std1(lo, hi, step):
                pool.wait_ge(mv1_done, hi)
                nc.gpsimd.tensor_tensor(rstd1[:, lo:hi], mv1[:, lo:hi, 1], eps[:, lo:hi], ALU.add
                                        ).then_inc(var1_done, 1)
                pool.wait_ge(var1_done, step)
                nc.gpsimd.tensor_tensor(rstd1[:, lo:hi], rstd1[:, lo:hi], half_neg[:, lo:hi], ALU.pow
                                        ).then_inc(rstd1_done, 1)

            def inverse_std2(j, p):
                pool.wait_ge(mv2_done, j + 1)
                nc.gpsimd.tensor_tensor(var2[:, p, :], mv2[:, p, :, 1], eps[:, 0:BT], ALU.add
                                        ).then_inc(var2_done, 1)
                pool.wait_ge(var2_done, j + 1)
                nc.gpsimd.tensor_tensor(rstd2[:, p, :], var2[:, p, :], half_neg[:, 0:BT], ALU.pow
                                        ).then_inc(rstd2_done, 1)

            def add_bias(i):
                bias = out_bias[:, :].rearrange("p (a d) -> p a d", a=1).broadcast_to([P, BT, D])
                nc.gpsimd.tensor_tensor(batch_tiles(x_bias, i), batch_tiles(x_all, i), bias, ALU.add
                                        ).then_inc(x_bias_ready, 1)

            pool.wait_ge(filled, 3)
            inverse_std1(0, BT, 1)
            pool.wait_ge(x_rest_in, 16)
            inverse_std1(BT, TILES, 2)
            pool.wait_ge(weights_ready, 1)
            add_bias(0)
            nc.gpsimd.memset(penalty[:, :, :, :], 0.0).then_inc(penalty_set, 1)
            pool.wait_ge(penalty_set, 1)
            nc.gpsimd.affine_select(out=penalty[:, :, :, :], in_=penalty[:, :, :, :], compare_op=ALU.not_equal,
                                    fill=PENALTY, base=0,
                                    pattern=[[-PER_CHUNK, CHUNKS], [-1, PER_CHUNK], [0, HIDDEN]],
                                    channel_multiplier=1).then_inc(penalty_set, 1)
            nc.gpsimd.iota(prefer[:, :, :], pattern=[[0, BT], [-1, EXPERTS]], base=EXPERTS,
                           channel_multiplier=0, allow_small_or_imprecise_dtypes=True).then_inc(prefer_set, 1)
            add_bias(1)
            pool.wait_ge(gate_up_in, 16)
            nc.gpsimd.tensor_copy(gate_up_hi[:, :, :, :], gate_up[:, :, :, :]).then_inc(split_hi, 1)
            inverse_std2(0, 0)
            pool.wait_ge(split_hi, 1)
            nc.gpsimd.tensor_tensor(gate_up_lo[:, :, :, :], gate_up[:, :, :, :],
                                    gate_up_hi[:, :, :, :].bitcast(F32), ALU.subtract).then_inc(split_ready, 1)
            with pool.Fori(LOOPED, BATCHES) as i:
                add_bias(i)
            with pool.Fori(0, PAIRS) as pair:
                for u in range(2):
                    inverse_std2(pair * 2 + (LOOPED + u - 1), 1 - u)
            inverse_std2(BATCHES - 1, 1)

        @block.scalar
        def _(act):
            act.dma_start(attn_sb[:, :], attn_w).then_inc(attn_in, 16)
            act.dma_start(bo_row[:, :], bo).then_inc(bo_in, 16)
            act.dma_start(gate_up[:, :, :, :], gate_up_t.rearrange("d (a c p) -> d a c p", a=2, p=P)
                          ).then_inc(gate_up_in, 16)
            act.dma_start(router_w[:, :], router_t).then_inc(router_in, 16)
            nc.scalar.preload_act_table(ACT.Exp)

            def keep_weight_products():
                products, biases = gate_up_banks
                act.wait_ge(weights_multiplied, 1)
                nc.scalar.activation(m_sb[:, :], products[:, 0:D], ACT.Copy)
                nc.scalar.activation(q_bias[:, :], products[:, D:D + 1], ACT.Copy, scale=SCALE)
                nc.scalar.activation(vo_sb[:, 0:D], products[:, 2 * D:3 * D], ACT.Copy)
                nc.scalar.activation(vo_sb[:, D:D + 1], products[:, 3 * D:3 * D + 1], ACT.Copy, scale=SCALE)
                nc.scalar.activation(qk_bias[:, :], biases[:, D:D + 1], ACT.Copy, scale=SCALE)
                nc.scalar.activation(out_bias[:, :], biases[:, 0:D], ACT.Copy).then_inc(weights_ready, 1)

            def normalise1(i, p):
                for t in range(BT):
                    tile = bass.ds(i * BT + t, 1)
                    last = nc.scalar.activation(xn[:, p, t, :], tile_of(x_all, i, t), ACT.Identity,
                                                scale=rstd1[:, tile], bias=shift1[:, tile])
                last.then_inc(xn_done, 1)

            def keep_xn(i, p):
                act.wait_ge(xn_turned, i + 1)
                nc.scalar.activation(xn_t[:, p, :], turn_bank[:, 0:SEQ], ACT.Copy).then_inc(xn_t_ready, 1)

            def keep_q(i, p):
                act.wait_ge(q_multiplied, i + 1)
                nc.scalar.activation(q_t[:, p, :], query_bank[:, 0:SEQ], ACT.Identity, scale=SCALE,
                                     bias=q_bias[:, 0:1]).then_inc(q_ready, 1)

            def keep_vo(i, p):
                act.wait_ge(vo_multiplied, i + 1)
                nc.scalar.activation(vo[:, p, :, :],
                                     probs_bank[:, 0:BT * (D + 1)].rearrange("p (t n) -> p t n", t=BT),
                                     ACT.Copy).then_inc(vo_ready, 1)

            def exponents(i, p):
                act.wait_ge(bias_done, i + 1)
                for t in range(BT):
                    last = nc.scalar.activation(probs[:, p, t, :], score_bank[:, cols(t, SEQ)], ACT.Exp,
                                                bias=exp_bias[:, p, t:t + 1], accum_out=row_sum[:, p, t:t + 1])
                last.then_inc(exp_done, 1)

            def keep_probs(i, p):
                act.wait_ge(probs_turned, i + 1)
                nc.scalar.activation(probs_t[:, p, :, :], probs_bank[:, :].rearrange("p (j i) -> p j i", j=BT),
                                     ACT.Copy).then_inc(probs_t_ready, 1)

            def keep_xm(j, p):
                act.wait_ge(xm_turned, j + 1)
                nc.scalar.activation(xm_t[:, p, :], turn_bank[:, 0:SEQ], ACT.Copy).then_inc(xm_t_ready, 1)

            def exp_of_top(j, p):
                act.wait_ge(top_done, j + 1)
                nc.scalar.activation(exp_top[:, p, :], top[:, p, :], ACT.Exp, scale=-1.0).then_inc(top_exp_done, 1)

            def weigh_xm(j, p):
                act.wait_ge(route_w_done, j + 1)
                for t in range(BT):
                    last = nc.scalar.activation(xs[:, p, t, :], xm[:, p, t, :], ACT.Copy,
                                                scale=route_w[:, p, t:t + 1])
                last.then_inc(xs_done, 1)

            def keep_unrouted(j, p):
                act.wait_ge(unrouted_turned, j + 1)
                nc.scalar.activation(unrouted_t[:, p, :], query_bank[0:EXPERTS, 0:SEQ], ACT.Copy
                                     ).then_inc(unrouted_t_ready, 1)

            def round_xs(j, p):
                act.wait_ge(xs_turned, j + 1)
                nc.scalar.activation(xs_hi[:, p, :], turn_bank[:, 0:SEQ], ACT.Copy).then_inc(xs_hi_ready, 1)

            def tanh_of_gate(h, c):
                act.wait_ge(gate_up_done, CHUNKS * h + c + 1)
                if c >= 2:
                    act.wait_ge(silu_done, CHUNKS * h + c - 1)
                nc.scalar.activation(tanh_g[:, c % 2, :], gate_up_banks[c % 2][:, 0:SEQ], ACT.Tanh, scale=0.5
                                     ).then_inc(tanh_done, 1)

            def attention(i, p):
                normalise1(i, p)
                keep_xn(i, p)
                keep_q(i, p)
                keep_vo(i, p)
                exponents(i, p)
                keep_probs(i, p)

            def routing(j, p):
                keep_xm(j, p)
                exp_of_top(j, p)
                weigh_xm(j, p)
                keep_unrouted(j, p)
                round_xs(j, p)

            act.wait_ge(shift1_done, 1)
            normalise1(0, 0)
            keep_xn(0, 0)
            keep_weight_products()
            keep_q(0, 0)
            keep_vo(0, 0)
            act.wait_ge(shift1_done, 2)
            exponents(0, 0)
            normalise1(1, 1)
            keep_xn(1, 1)
            keep_probs(0, 0)
            keep_q(1, 1)
            keep_vo(1, 1)
            exponents(1, 1)
            keep_xm(0, 0)
            keep_probs(1, 1)
            exp_of_top(0, 0)
            weigh_xm(0, 0)
            keep_unrouted(0, 0)
            round_xs(0, 0)
            with act.Fori(0, PAIRS) as pair:
                for p in range(2):
                    i, q = pair * 2 + (LOOPED + p), 1 - p
                    j, h = pair * 2 + (LOOPED + p - 1), pair * 2 + (LOOPED + p - 2)
                    normalise1(i, p)
                    tanh_of_gate(h, 0)
                    keep_xn(i, p)
                    tanh_of_gate(h, 1)
                    keep_q(i, p)
                    keep_vo(i, p)
                    keep_xm(j, q)
                    tanh_of_gate(h, 2)
                    tanh_of_gate(h, 3)
                    exp_of_top(j, q)
                    exponents(i, p)
                    weigh_xm(j, q)
                    keep_probs(i, p)
                    keep_unrouted(j, q)
                    round_xs(j, q)
            last_batch = BATCHES - 1
            tanh_of_gate(last_batch - 1, 0)
            tanh_of_gate(last_batch - 1, 1)
            keep_xm(last_batch, 1)
            tanh_of_gate(last_batch - 1, 2)
            exp_of_top(last_batch, 1)
            weigh_xm(last_batch, 1)
            tanh_of_gate(last_batch - 1, 3)
            keep_unrouted(last_batch, 1)
            round_xs(last_batch, 1)
            for c in range(CHUNKS):
                tanh_of_gate(last_batch, c)

        @block.vector
        def _(dve):
            nc.vector.memset(eps[:, :], EPS).then_inc(filled, 1)
            nc.vector.memset(half_neg[:, :], -0.5).then_inc(filled, 1)
            nc.vector.memset(ones[:, :], 1.0).then_inc(filled, 1)

            def statistics1(lo, hi):
                for t in range(lo, hi):
                    nc.vector.bn_stats(stats1[:, t, :], x_all[:, t, :]).then_inc(stats1_done, 1)
                for t in range(lo, hi):
                    dve.wait_ge(stats1_done, t + 1)
                    nc.vector.bn_aggr(mv1[:, t, :], stats1[:, t, :]).then_inc(mv1_done, 1)

            def mean_shift(lo, hi, step):
                dve.wait_ge(rstd1_done, step)
                nc.vector.scalar_tensor_tensor(out=shift1[:, lo:hi], in0=mv1[:, lo:hi, 0], scalar=-1.0,
                                               in1=rstd1[:, lo:hi], op0=ALU.mult, op1=ALU.mult
                                               ).then_inc(shift1_done, 1)

            def row_shift(i, p):
                dve.wait_ge(vo_ready, i + 1)
                nc.vector.tensor_scalar(shift[:, p, :], vo[:, p, :, D], qk_bias[:, 0:1], None, ALU.add
                                        ).then_inc(shift_done, 1)

            def row_maxima(i, p):
                dve.wait_ge(scored, i + 1)
                nc.vector.tensor_reduce(neg_max[:, p, :], score_bank[:, :].rearrange("p (t j) -> p t j", t=BT),
                                        AX_X, ALU.max, negate=True).then_inc(max_done, 1)
                dve.wait_ge(shift_done, i + 1)
                dve.wait_ge(max_done, i + 1)
                nc.vector.tensor_tensor(neg_max_less[:, p, :], neg_max[:, p, :], shift[:, p, :], ALU.subtract
                                        ).then_inc(less_done, 1)
                dve.wait_ge(less_done, i + 1)
                nc.vector.tensor_tensor(exp_bias[:, p, :], neg_max_less[:, p, :], shift[:, p, :], ALU.add
                                        ).then_inc(bias_done, 1)

            def row_inverse(i, p):
                dve.wait_ge(exp_done, i + 1)
                nc.vector.reciprocal(row_inv[:, p, :], row_sum[:, p, :]).then_inc(row_inv_done, 1)

            def add_attention(i, p):
                dve.wait_ge(x_bias_ready, i + 1)
                dve.wait_ge(row_inv_done, i + 1)
                dve.wait_ge(attended, i + 1)
                for t in range(BT):
                    last = nc.vector.scalar_tensor_tensor(
                        out=tile_of(x_mid, i, t), in0=attn_bank[:, cols(t)], scalar=row_inv[:, p, t:t + 1],
                        in1=tile_of(x_bias, i, t), op0=ALU.mult, op1=ALU.add)
                last.then_inc(x_mid_done, 1)

            def carry_wait():
                nc.vector.memset(scratch[:, :], 0.0)

            def statistics2(j, p):
                dve.wait_ge(x_mid_done, j + 1)
                carry_wait()
                for t in range(BT):
                    last = nc.vector.bn_stats(stats2[:, p, t, :], tile_of(x_mid, j, t))
                last.then_inc(stats2_done, 1)
                dve.wait_ge(stats2_done, j + 1)
                carry_wait()
                for t in range(BT):
                    last = nc.vector.bn_aggr(mv2[:, p, t, :], stats2[:, p, t, :])
                last.then_inc(mv2_done, 1)

            def normalise2(j, p):
                dve.wait_ge(rstd2_done, j + 1)
                for t in range(BT):
                    last = nc.vector.tensor_scalar(xm[:, p, t, :], tile_of(x_mid, j, t), mv2[:, p, t, 0:1],
                                                   rstd2[:, p, t:t + 1], ALU.subtract, ALU.mult)
                last.then_inc(xm_done, 1)

            def route(j, p):
                logits = attn_bank[:, 0:BT * EXPERTS].rearrange("p (t e) -> p t e", t=BT)

                def spread(v):
                    return v[:, p, :].rearrange("p (t a) -> p t a", a=1).broadcast_to([P, BT, EXPERTS])
                dve.wait_ge(logits_done, j + 1)
                nc.vector.tensor_reduce(top[:, p, :], logits, AX_X, ALU.max).then_inc(top_done, 1)
                dve.wait_ge(top_done, j + 1)
                nc.vector.tensor_tensor(is_top[:, p, :, :], logits, spread(top), ALU.is_equal
                                        ).then_inc(is_top_done, 1)
                dve.wait_ge(is_top_done, j + 1)
                nc.vector.tensor_tensor(ranked[:, p, :, :], is_top[:, p, :, :], prefer[:, :, :], ALU.mult
                                        ).then_inc(ranked_done, 1)
                dve.wait_ge(top_exp_done, j + 1)
                nc.vector.tensor_scalar(exp_top1[:, p, :], exp_top[:, p, :], 1.0, None, ALU.add
                                        ).then_inc(exp_top1_done, 1)
                dve.wait_ge(ranked_done, j + 1)
                nc.vector.tensor_reduce(first[:, p, :], ranked[:, p, :, :], AX_X, ALU.max).then_inc(first_done, 1)
                dve.wait_ge(exp_top1_done, j + 1)
                nc.vector.reciprocal(route_w[:, p, :], exp_top1[:, p, :]).then_inc(route_w_done, 1)
                dve.wait_ge(first_done, j + 1)
                nc.vector.tensor_tensor(unrouted[:, p, :, :], ranked[:, p, :, :], spread(first), ALU.not_equal
                                        ).then_inc(unrouted_done, 1)

            def rest_of_xs(j, p):
                dve.wait_ge(xs_hi_ready, j + 1)
                nc.vector.tensor_tensor(xs_lo[:, p, :], turn_bank[:, 0:SEQ], xs_hi[:, p, :].bitcast(F32),
                                        ALU.subtract).then_inc(xs_lo_ready, 1)

            def hidden(h, p, c):
                gate_up_bank = gate_up_banks[c % 2]
                dve.wait_ge(tanh_done, CHUNKS * h + c + 1)
                nc.vector.scalar_tensor_tensor(out=silu2[:, c % 2, :], in0=tanh_g[:, c % 2, :], scalar=1.0,
                                               in1=gate_up_bank[:, 0:SEQ], op0=ALU.add, op1=ALU.mult
                                               ).then_inc(silu_done, 1)
                dve.wait_ge(silu_done, CHUNKS * h + c + 1)
                nc.vector.scalar_tensor_tensor(out=hid_t[:, p, c, :], in0=gate_up_bank[:, SEQ:2 * SEQ], scalar=0.5,
                                               in1=silu2[:, c % 2, :], op0=ALU.mult, op1=ALU.mult
                                               ).then_inc(hid_done, 1)

            def add_experts(h):
                dve.wait_ge(down_done, h + 1)
                nc.vector.tensor_tensor(batch_tiles(y_all, h),
                                        down_bank[:, 0:BT * D].rearrange("p (t d) -> p t d", t=BT),
                                        batch_tiles(x_mid, h), ALU.add).then_inc(y_done, 1)

            dve.wait_ge(x_first_in, 16)
            statistics1(0, BT)
            mean_shift(0, BT, 1)
            dve.wait_ge(attn_in, 16)
            nc.vector.tensor_copy(bv_wide[:, :], attn_sb[:, BV:BV + 1].broadcast_to([P, P])).then_inc(wide_set, 1)
            nc.vector.tensor_copy(bq_wide[:, :], attn_sb[:, BQ:BQ + 1].broadcast_to([P, P])).then_inc(wide_set, 1)
            dve.wait_ge(x_rest_in, 16)
            statistics1(BT, TILES)
            mean_shift(BT, TILES, 2)
            row_shift(0, 0)
            row_maxima(0, 0)
            row_inverse(0, 0)
            row_shift(1, 1)
            add_attention(0, 0)
            statistics2(0, 0)
            row_maxima(1, 1)
            normalise2(0, 0)
            row_inverse(1, 1)
            dve.wait_ge(prefer_set, 1)
            route(0, 0)
            add_attention(1, 1)
            rest_of_xs(0, 0)
            with dve.Fori(0, PAIRS) as pair:
                for p in range(2):
                    i, q = pair * 2 + (LOOPED + p), 1 - p
                    j, h = pair * 2 + (LOOPED + p - 1), pair * 2 + (LOOPED + p - 2)
                    statistics2(j, q)
                    hidden(h, p, 0)
                    normalise2(j, q)
                    hidden(h, p, 1)
                    row_shift(i, p)
                    hidden(h, p, 2)
                    hidden(h, p, 3)
                    route(j, q)
                    row_maxima(i, p)
                    row_inverse(i, p)
                    add_experts(h)
                    rest_of_xs(j, q)
                    add_attention(i, p)
            last_batch = BATCHES - 1
            statistics2(last_batch, 1)
            hidden(last_batch - 1, 0, 0)
            normalise2(last_batch, 1)
            hidden(last_batch - 1, 0, 1)
            hidden(last_batch - 1, 0, 2)
            route(last_batch, 1)
            hidden(last_batch - 1, 0, 3)
            rest_of_xs(last_batch, 1)
            add_experts(last_batch - 1)
            for c in range(CHUNKS):
                hidden(last_batch, 1, c)
            add_experts(last_batch)

        @block.tensor
        def _(pe):
            def weight_products():
                products, biases = gate_up_banks
                wq, wk, wv, wo_t = (attn_sb[:, w:w + D] for w in (WQ, WK, WV, WOT))
                pe.wait_ge(attn_in, 16)
                nc.tensor.matmul(products[:, 0:D], wq, wk, start=True, stop=True)
                nc.tensor.matmul(products[:, D:D + 1], wk, attn_sb[:, BQ:BQ + 1], start=True, stop=True)
                nc.tensor.matmul(products[:, 2 * D:3 * D], wv, wo_t, start=True, stop=True)
                nc.tensor.matmul(products[:, 3 * D:3 * D + 1], wq, attn_sb[:, BK:BK + 1], start=True, stop=True)
                pe.wait_ge(wide_set, 2)
                nc.tensor.matmul(biases[:, D:D + 1], bq_wide[:, :], attn_sb[:, BK:BK + 1], start=True, stop=True)
                pe.wait_ge(filled, 3)
                pe.wait_ge(bo_in, 16)
                nc.tensor.matmul(biases[:, 0:D], bv_wide[:, :], wo_t, start=True, stop=False)
                nc.tensor.matmul(biases[:, 0:D], ones[0:1, :], bo_row[:, :], start=False, stop=True
                                 ).then_inc(weights_multiplied, 1)

            def turn(source, p, done):
                for t in range(BT):
                    last = nc.tensor.transpose(turn_bank[:, cols(t)], source[:, p, t, :], ident[:, :])
                last.then_inc(done, 1)

            def turn_xn(i, p):
                pe.wait_ge(xn_done, i + 1)
                turn(xn, p, xn_turned)

            def query(i, p):
                pe.wait_ge(xn_t_ready, i + 1)
                nc.tensor.matmul(query_bank[:, 0:SEQ], m_sb[:, :], xn_t[:, p, :], start=True, stop=True
                                 ).then_inc(q_multiplied, 1)

            def value(i, p):
                pe.wait_ge(xn_t_ready, i + 1)
                for t in range(BT):
                    last = nc.tensor.matmul(probs_bank[:, cols(t, D + 1)], xn_t[:, p, cols(t)], vo_sb[:, :],
                                            start=True, stop=True)
                last.then_inc(vo_multiplied, 1)

            def scores(i, p):
                pe.wait_ge(q_ready, i + 1)
                for t in range(BT):
                    last = nc.tensor.matmul(score_bank[:, cols(t, SEQ)], q_t[:, p, cols(t)], xn_t[:, p, :],
                                            start=True, stop=True)
                last.then_inc(scored, 1)

            def turn_probs(i, p):
                pe.wait_ge(vo_ready, i + 1)
                pe.wait_ge(exp_done, i + 1)
                for j in range(BT):
                    for t in range(BT):
                        last = nc.tensor.transpose(probs_bank[:, j * SEQ + t * P:j * SEQ + (t + 1) * P],
                                                   probs[:, p, t, cols(j)], ident[:, :])
                last.then_inc(probs_turned, 1)

            def attend(i, p):
                pe.wait_ge(probs_t_ready, i + 1)
                for t in range(BT):
                    for j in range(BT):
                        last = nc.tensor.matmul(attn_bank[:, cols(t)], probs_t[:, p, j, cols(t)],
                                                vo[:, p, j, 0:D], start=(j == 0), stop=(j == BT - 1))
                last.then_inc(attended, 1)

            def turn_xm(j, p):
                pe.wait_ge(xm_done, j + 1)
                turn(xm, p, xm_turned)

            def logits(j, p):
                pe.wait_ge(xm_t_ready, j + 1)
                for t in range(BT):
                    last = nc.tensor.matmul(attn_bank[:, cols(t, EXPERTS)], xm_t[:, p, cols(t)],
                                            router_w[:, :], start=True, stop=True)
                last.then_inc(logits_done, 1)

            def turn_unrouted(j, p):
                pe.wait_ge(unrouted_done, j + 1)
                for t in range(BT):
                    last = nc.tensor.transpose(query_bank[0:EXPERTS, cols(t)], unrouted[:, p, t, :], ident[:, :])
                last.then_inc(unrouted_turned, 1)

            def turn_xs(j, p):
                pe.wait_ge(xs_done, j + 1)
                turn(xs, p, xs_turned)

            def gate_and_up(h, p, c):
                target = gate_up_banks[c % 2]
                if c == 0:
                    pe.wait_ge(xs_lo_ready, h + 1)
                    pe.wait_ge(unrouted_t_ready, h + 1)
                if c >= 2:
                    pe.wait_ge(hid_done, CHUNKS * h + c - 1)
                for which in range(2):
                    half = target[:, cols(which, SEQ)]
                    w_hi, w_lo = gate_up_hi[:, which, c, :], gate_up_lo[:, which, c, :]
                    if which == 0:
                        nc.tensor.matmul(half, penalty[:, c, :, :].rearrange("e s i -> e (s i)"),
                                         unrouted_t[:, p, :], start=True, stop=False)
                    nc.tensor.matmul(half, w_lo, xs_hi[:, p, :], start=(which == 1), stop=False)
                    nc.tensor.matmul(half, w_hi, xs_lo[:, p, :], start=False, stop=False)
                    last = nc.tensor.matmul(half, w_hi, xs_hi[:, p, :], start=False, stop=True)
                last.then_inc(gate_up_done, 1)

            def down(h, p, t):
                if t == 0:
                    pe.wait_ge(hid_done, CHUNKS * h + CHUNKS)
                for c in range(CHUNKS):
                    last = nc.tensor.matmul(down_bank[:, cols(t)], hid_t[:, p, c, cols(t)], down_w[:, c, :],
                                            start=(c == 0), stop=(c == CHUNKS - 1))
                if t == BT - 1:
                    last.then_inc(down_done, 1)

            pe.wait_ge(ident_set, 2)
            turn_xn(0, 0)
            weight_products()
            pe.wait_ge(weights_ready, 1)
            query(0, 0)
            value(0, 0)
            scores(0, 0)
            turn_xn(1, 1)
            query(1, 1)
            turn_probs(0, 0)
            scores(1, 1)
            attend(0, 0)
            pe.wait_ge(probs_t_ready, 1)
            value(1, 1)
            turn_xm(0, 0)
            pe.wait_ge(router_in, 16)
            turn_probs(1, 1)
            pe.wait_ge(x_mid_done, 1)
            logits(0, 0)
            pe.wait_ge(top_done, 1)
            turn_unrouted(0, 0)
            attend(1, 1)
            turn_xs(0, 0)
            pe.wait_ge(split_ready, 1)
            pe.wait_ge(penalty_set, 2)
            pe.wait_ge(down_in, 16)
            with pe.Fori(0, PAIRS) as pair:
                for p in range(2):
                    i, q = pair * 2 + (LOOPED + p), 1 - p
                    j, h = pair * 2 + (LOOPED + p - 1), pair * 2 + (LOOPED + p - 2)
                    gate_and_up(h, p, 0)
                    turn_xn(i, p)
                    gate_and_up(h, p, 1)
                    query(i, p)
                    value(i, p)
                    turn_xm(j, q)
                    gate_and_up(h, p, 2)
                    gate_and_up(h, p, 3)
                    logits(j, q)
                    scores(i, p)
                    down(h, p, 0)
                    down(h, p, 1)
                    turn_probs(i, p)
                    turn_unrouted(j, q)
                    turn_xs(j, q)
                    attend(i, p)
            last_batch = BATCHES - 1
            gate_and_up(last_batch - 1, 0, 0)
            gate_and_up(last_batch - 1, 0, 1)
            turn_xm(last_batch, 1)
            gate_and_up(last_batch - 1, 0, 2)
            logits(last_batch, 1)
            gate_and_up(last_batch - 1, 0, 3)
            turn_unrouted(last_batch, 1)
            turn_xs(last_batch, 1)
            down(last_batch - 1, 0, 0)
            down(last_batch - 1, 0, 1)
            for c in range(CHUNKS):
                gate_and_up(last_batch, 1, c)
            down(last_batch, 1, 0)
            down(last_batch, 1, 1)


def kernel(**inputs):
    import numpy as np
    import concourse.bacc as bacc
    from concourse.bass_utils import run_bass_kernel_spmd

    def f32(name):
        return np.asarray(inputs[name])

    def column(name):
        return f32(name).reshape(D, 1)

    arrays = {
        "x": f32("L0_attn_x"),
        "attn_w": np.concatenate([f32("L0_attn_w_q"), f32("L0_attn_w_k"), f32("L0_attn_w_v"), f32("L0_attn_w_out").T,
                                  column("L0_attn_b_q"), column("L0_attn_b_k"), column("L0_attn_b_v")], axis=1),
        "bo": f32("L0_attn_b_out").reshape(1, D),
        "gate_up_t": np.concatenate([f32("L0_ffn_w_gate").reshape(EXPERTS * HIDDEN, D).T,
                                     f32("L0_ffn_w_up").reshape(EXPERTS * HIDDEN, D).T], axis=1),
        "down_t": f32("L0_ffn_w_down").transpose(0, 2, 1).reshape(EXPERTS * HIDDEN, D),
        "router_t": f32("L0_ffn_gate_w").T,
    }
    nc = bacc.Bacc("TRN2", target_bir_lowering=False, num_devices=1)
    sent, args = {}, []
    for name, a in arrays.items():
        a = np.ascontiguousarray(a)
        sent[f"in_{name}"] = a
        args.append(nc.dram_tensor(f"in_{name}", a.shape, mybir.dt.from_np(a.dtype), kind="ExternalInput").ap())
    out = nc.dram_tensor("out_x", [BATCHES, SEQ, D], F32, kind="ExternalOutput").ap()
    layer_kernel(nc, *args, out)
    result = run_bass_kernel_spmd(nc, [sent], core_ids=[0])
    return result.results[0]["out_x"]
```

```python
from contextlib import ExitStack

import concourse.bass as bass
from concourse import mybir

F32 = mybir.dt.float32
F32R = mybir.dt.float32r
BF16 = mybir.dt.bfloat16
ALU = mybir.AluOpType
ACT = mybir.ActivationFunctionType
AX_X = mybir.AxisListType.X

P = 128
D = 128
BATCHES, SEQ = 8, 256
EXPERTS, HIDDEN = 8, 64
BT = SEQ // P
TILES = BATCHES * BT
CHUNKS = EXPERTS * HIDDEN // P
PER_CHUNK = P // HIDDEN
SCALE = float(D) ** -0.5
EPS = 1e-5
PENALTY = -1e30
LOOPED = 4
AHEAD = 2 * BT
PAIRS = (BATCHES - LOOPED) // 2
LAST = BATCHES - 1

WQ, WK, WV, WOT, BQ, BK, BV = 0, D, 2 * D, 3 * D, 4 * D, 4 * D + 1, 4 * D + 2
ATTN_COLS = 4 * D + 3


def layer_kernel(nc, x, attn_w, bo, gate_up_t, down_t, router_t, out):
    with ExitStack() as ctx:
        def sb(name, shape, dt=F32):
            return ctx.enter_context(nc.sbuf_tensor(name, shape, dt))

        def bank(name):
            return ctx.enter_context(nc.psum_tensor(name, [P, 512], F32))

        def sem(name):
            return ctx.enter_context(nc.semaphore(name))

        x_all = sb("x_all", [P, TILES + BT, D])
        x_bias = sb("x_bias", [P, TILES, D])
        x_mid = sb("x_mid", [P, TILES, D])
        y_all = sb("y_all", [P, TILES, D])
        attn_sb = sb("attn_sb", [P, ATTN_COLS])
        bo_row = sb("bo_row", [1, D])
        gate_up = sb("gate_up", [P, 2, CHUNKS, P])
        gate_up_hi = sb("gate_up_hi", [P, 2, CHUNKS, P], F32R)
        gate_up_lo = sb("gate_up_lo", [P, 2, CHUNKS, P], F32R)
        down_w = sb("down_w", [P, CHUNKS, D])
        router_w = sb("router_w", [P, EXPERTS])
        ident = sb("ident", [P, P])
        ones = sb("ones", [P, P])
        bv_wide = sb("bv_wide", [P, P])
        bq_wide = sb("bq_wide", [P, P])
        prefer = sb("prefer", [P, BT, EXPERTS])
        penalty = sb("penalty", [EXPERTS, CHUNKS, PER_CHUNK, HIDDEN], BF16)
        scratch = sb("scratch", [1, 1])
        eps = sb("eps", [P, TILES])
        half_neg = sb("half_neg", [P, TILES])
        m_sb = sb("m_sb", [P, D])
        q_bias = sb("q_bias", [P, 1])
        vo_sb = sb("vo_sb", [P, D + 1])
        out_bias = sb("out_bias", [P, D])
        qk_bias = sb("qk_bias", [P, 1])
        stats1 = sb("stats1", [P, TILES, 6])
        mv1 = sb("mv1", [P, TILES, 2])
        rstd1 = sb("rstd1", [P, TILES + BT])
        shift1 = sb("shift1", [P, TILES + BT])

        xn = sb("xn", [P, 2, BT, D])
        xn_centred = sb("xn_centred", [P, BT, D])
        xn_t = sb("xn_t", [P, 2, SEQ])
        q_t = sb("q_t", [P, 2, SEQ])
        vo = sb("vo", [P, 2, BT, D + 1])
        shift = sb("shift", [P, 2, BT])
        neg_max = sb("neg_max", [P, 2, BT])
        neg_max_less = sb("neg_max_less", [P, 2, BT])
        exp_bias = sb("exp_bias", [P, 2, BT])
        probs = sb("probs", [P, 2, BT, SEQ])
        row_sum = sb("row_sum", [P, 2, BT])
        row_inv = sb("row_inv", [P, 2, BT])
        probs_t = sb("probs_t", [P, 2, BT, SEQ])
        stats2 = sb("stats2", [P, 2, BT, 6])
        mv2 = sb("mv2", [P, 2, BT, 2])
        var2 = sb("var2", [P, 2, BT])
        rstd2 = sb("rstd2", [P, 2, BT])
        centred = sb("centred", [P, 2, BT, D])
        xm = sb("xm", [P, 2, BT, D])
        xm_t = sb("xm_t", [P, 2, SEQ])
        top = sb("top", [P, 2, BT])
        is_top = sb("is_top", [P, 2, BT, EXPERTS])
        ranked = sb("ranked", [P, 2, BT, EXPERTS])
        first = sb("first", [P, 2, BT])
        unrouted = sb("unrouted", [P, 2, BT, EXPERTS])
        exp_top = sb("exp_top", [P, 2, BT])
        exp_top1 = sb("exp_top1", [P, 2, BT])
        route_w = sb("route_w", [P, 2, BT])
        xs = sb("xs", [P, 2, BT, D])
        xs_hi = sb("xs_hi", [P, 2, SEQ], F32R)
        xs_lo = sb("xs_lo", [P, 2, SEQ], F32R)
        unrouted_t = sb("unrouted_t", [EXPERTS, 2, SEQ], BF16)
        hid_t = sb("hid_t", [P, 2, CHUNKS, SEQ])
        tanh_g = sb("tanh_g", [P, 2, SEQ])
        silu2 = sb("silu2", [P, 2, SEQ])

        turn_bank = bank("turn_bank")
        query_bank = bank("query_bank")
        score_bank = bank("score_bank")
        probs_bank = bank("probs_bank")
        attn_bank = bank("attn_bank")
        even_bank, odd_bank = bank("gate_up_even"), bank("gate_up_odd")
        down_bank = bank("down_bank")
        loop_banks = (even_bank, odd_bank, attn_bank, even_bank)
        last_down_banks = (turn_bank, attn_bank)
        wide_banks = (even_bank, odd_bank, score_bank, probs_bank)

        x_first_in, x_rest_in = sem("x_first_in"), sem("x_rest_in")
        attn_in, bo_in, gate_up_in, down_in, router_in = (
            sem("attn_in"), sem("bo_in"), sem("gate_up_in"), sem("down_in"), sem("router_in"))
        out_stored = sem("out_stored")
        filled, wide_set = sem("filled"), sem("wide_set")
        ident_set, penalty_set, prefer_set = sem("ident_set"), sem("penalty_set"), sem("prefer_set")
        m_multiplied, vo_w_multiplied = sem("m_multiplied"), sem("vo_w_multiplied")
        qk_bias_multiplied, out_bias_multiplied = sem("qk_bias_multiplied"), sem("out_bias_multiplied")
        m_ready, vo_w_ready = sem("m_ready"), sem("vo_w_ready")
        qk_bias_ready, out_bias_ready = sem("qk_bias_ready"), sem("out_bias_ready")
        split_hi, split_ready = sem("split_hi"), sem("split_ready")
        stats1_done, mv1_done, var1_done, rstd1_done, shift1_done = (
            sem("stats1_done"), sem("mv1_done"), sem("var1_done"), sem("rstd1_done"), sem("shift1_done"))
        xn_centred_done = sem("xn_centred_done")
        xn_done, xn_turned, xn_t_ready = sem("xn_done"), sem("xn_turned"), sem("xn_t_ready")
        q_multiplied, q_ready = sem("q_multiplied"), sem("q_ready")
        vo_multiplied, vo_ready = sem("vo_multiplied"), sem("vo_ready")
        scored, max_done, less_done, bias_done, exp_done = (
            sem("scored"), sem("max_done"), sem("less_done"), sem("bias_done"), sem("exp_done"))
        shift_done, row_inv_done, x_bias_ready = sem("shift_done"), sem("row_inv_done"), sem("x_bias_ready")
        probs_turned, probs_t_ready = sem("probs_turned"), sem("probs_t_ready")
        attended, x_mid_done = sem("attended"), sem("x_mid_done")
        stats2_done, mv2_done, var2_done, rstd2_done, xm_done = (
            sem("stats2_done"), sem("mv2_done"), sem("var2_done"), sem("rstd2_done"), sem("xm_done"))
        centred_done = sem("centred_done")
        xm_turned, xm_t_ready = sem("xm_turned"), sem("xm_t_ready")
        logits_done, top_done, top_exp_done = sem("logits_done"), sem("top_done"), sem("top_exp_done")
        is_top_done, ranked_done, first_done, unrouted_done = (
            sem("is_top_done"), sem("ranked_done"), sem("first_done"), sem("unrouted_done"))
        exp_top1_done, route_w_done = sem("exp_top1_done"), sem("route_w_done")
        unrouted_turned, unrouted_t_ready = sem("unrouted_turned"), sem("unrouted_t_ready")
        xs_done, xs_turned, xs_hi_ready, xs_lo_ready = (
            sem("xs_done"), sem("xs_turned"), sem("xs_hi_ready"), sem("xs_lo_ready"))
        gate_up_done, tanh_done, silu_done, hid_done = (
            sem("gate_up_done"), sem("tanh_done"), sem("silu_done"), sem("hid_done"))
        down_done, y_done = sem("down_done"), sem("y_done")

        x_dram = x.rearrange("b (h p) d -> p (b h) d", p=P)
        out_dram = out.rearrange("b (h p) d -> p (b h) d", p=P)

        def batch_tiles(buffer, b):
            return buffer[:, bass.ds(b * BT, BT), :]

        def tile_of(buffer, b, t):
            return buffer[:, bass.ds(b * BT + t, 1), :].rearrange("p a d -> p (a d)")

        def cols(t, width=P):
            return slice(t * width, (t + 1) * width)

        block = ctx.enter_context(nc.Block())

        @block.sync
        def _(sp):
            sp.dma_start(x_all[:, 0:AHEAD, :], x_dram[:, 0:AHEAD, :]).then_inc(x_first_in, 16)
            sp.dma_start(x_all[:, AHEAD:TILES, :], x_dram[:, AHEAD:TILES, :]).then_inc(x_rest_in, 16)
            sp.dma_start(down_w[:, :, :], down_t.rearrange("(c p) d -> p c d", p=P)).then_inc(down_in, 16)
            with sp.Fori(0, BATCHES - 1) as h:
                sp.wait_ge(y_done, h + 1)
                sp.dma_start(batch_tiles(out_dram, h), batch_tiles(y_all, h)).then_inc(out_stored, 16)
            sp.wait_ge(y_done, BATCHES - 1 + BT)
            sp.dma_start(batch_tiles(out_dram, LAST), batch_tiles(y_all, LAST)).then_inc(out_stored, 16)
            sp.wait_ge(out_stored, 16 * BATCHES)

        @block.gpsimd
        def _(pool):
            nc.gpsimd.memset(ident[:, :], 0.0).then_inc(ident_set, 1)
            pool.wait_ge(ident_set, 1)
            nc.gpsimd.affine_select(out=ident[:, :], in_=ident[:, :], compare_op=ALU.not_equal, fill=1.0,
                                    base=0, pattern=[[-1, P]], channel_multiplier=1).then_inc(ident_set, 1)

            def inverse_std1(lo, hi, step):
                pool.wait_ge(mv1_done, hi)
                nc.gpsimd.tensor_tensor(rstd1[:, lo:hi], mv1[:, lo:hi, 1], eps[:, lo:hi], ALU.add
                                        ).then_inc(var1_done, 1)
                pool.wait_ge(var1_done, step)
                nc.gpsimd.tensor_tensor(rstd1[:, lo:hi], rstd1[:, lo:hi], half_neg[:, lo:hi], ALU.pow
                                        ).then_inc(rstd1_done, 1)

            def inverse_std2(j, p):
                pool.wait_ge(mv2_done, j + 1)
                nc.gpsimd.tensor_tensor(var2[:, p, :], mv2[:, p, :, 1], eps[:, 0:BT], ALU.add
                                        ).then_inc(var2_done, 1)
                pool.wait_ge(var2_done, j + 1)
                nc.gpsimd.tensor_tensor(rstd2[:, p, :], var2[:, p, :], half_neg[:, 0:BT], ALU.pow
                                        ).then_inc(rstd2_done, 1)

            def spread(v):
                return v.rearrange("p (t a) -> p t a", a=1).broadcast_to([P, BT, D])

            def normalise1(i, p):
                tiles = slice(i * BT, (i + 1) * BT)
                nc.gpsimd.tensor_tensor(xn_centred[:, :, :], x_all[:, tiles, :], spread(mv1[:, tiles, 0]),
                                        ALU.subtract).then_inc(xn_centred_done, 1)
                pool.wait_ge(xn_centred_done, 1)
                pool.wait_ge(xn_turned, i - 1)
                nc.gpsimd.tensor_tensor(xn[:, p, :, :], xn_centred[:, :, :], spread(rstd1[:, tiles]),
                                        ALU.mult).then_inc(xn_done, 1)

            def normalise2(j, p):
                nc.gpsimd.tensor_tensor(centred[:, p, :, :], batch_tiles(x_mid, j), spread(mv2[:, p, :, 0]),
                                        ALU.subtract).then_inc(centred_done, 1)
                pool.wait_ge(centred_done, j)
                nc.gpsimd.tensor_tensor(xm[:, p, :, :], centred[:, p, :, :], spread(rstd2[:, p, :]),
                                        ALU.mult).then_inc(xm_done, 1)

            def add_bias(i):
                bias = out_bias[:, :].rearrange("p (a d) -> p a d", a=1).broadcast_to([P, BT, D])
                nc.gpsimd.tensor_tensor(batch_tiles(x_bias, i), batch_tiles(x_all, i), bias, ALU.add
                                        ).then_inc(x_bias_ready, 1)

            pool.wait_ge(filled, 3)
            inverse_std1(0, BT, 1)
            inverse_std1(BT, AHEAD, 2)
            nc.gpsimd.memset(penalty[:, :, :, :], 0.0).then_inc(penalty_set, 1)
            pool.wait_ge(penalty_set, 1)
            nc.gpsimd.affine_select(out=penalty[:, :, :, :], in_=penalty[:, :, :, :], compare_op=ALU.not_equal,
                                    fill=PENALTY, base=0,
                                    pattern=[[-PER_CHUNK, CHUNKS], [-1, PER_CHUNK], [0, HIDDEN]],
                                    channel_multiplier=1).then_inc(penalty_set, 1)
            nc.gpsimd.iota(prefer[:, :, :], pattern=[[0, BT], [-1, EXPERTS]], base=EXPERTS,
                           channel_multiplier=0, allow_small_or_imprecise_dtypes=True).then_inc(prefer_set, 1)
            inverse_std1(AHEAD, AHEAD + BT, 3)
            inverse_std1(AHEAD + BT, TILES, 4)
            pool.wait_ge(x_rest_in, 16)
            pool.wait_ge(split_hi, 1)
            nc.gpsimd.tensor_tensor(gate_up_lo[:, :, :, :], gate_up[:, :, :, :],
                                    gate_up_hi[:, :, :, :].bitcast(F32), ALU.subtract).then_inc(split_ready, 1)
            pool.wait_ge(out_bias_ready, 1)
            for b in range(LOOPED):
                add_bias(b)
            inverse_std2(0, 0)
            pool.wait_ge(xn_done, LOOPED)
            normalise1(LOOPED, 0)
            for b in range(1, LOOPED - 1):
                inverse_std2(b, b % 2)
                normalise2(b, b % 2)
            with pool.Fori(0, PAIRS) as pair:
                for p in range(2):
                    add_bias(pair * 2 + (LOOPED + p))
                    inverse_std2(pair * 2 + (LOOPED + p - 1), 1 - p)
                    normalise2(pair * 2 + (LOOPED + p - 1), 1 - p)
            inverse_std2(BATCHES - 1, 1)
            normalise2(BATCHES - 1, 1)

        @block.scalar
        def _(act):
            act.dma_start(attn_sb[:, :], attn_w).then_inc(attn_in, 16)
            act.dma_start(bo_row[:, :], bo).then_inc(bo_in, 16)
            act.dma_start(gate_up[:, :, :, :], gate_up_t.rearrange("d (a c p) -> d a c p", a=2, p=P)
                          ).then_inc(gate_up_in, 16)
            act.dma_start(router_w[:, :], router_t).then_inc(router_in, 16)
            nc.scalar.preload_act_table(ACT.Exp)

            def keep_vo_product():
                act.wait_ge(vo_w_multiplied, 1)
                nc.scalar.activation(vo_sb[:, 0:D], odd_bank[:, 0:D], ACT.Copy)
                nc.scalar.activation(vo_sb[:, D:D + 1], odd_bank[:, D:D + 1], ACT.Copy, scale=SCALE
                                     ).then_inc(vo_w_ready, 1)

            def keep_qk_bias():
                act.wait_ge(qk_bias_multiplied, 1)
                nc.scalar.activation(qk_bias[:, :], even_bank[:, 0:1], ACT.Copy, scale=SCALE).then_inc(qk_bias_ready, 1)

            def keep_out_bias():
                act.wait_ge(out_bias_multiplied, 1)
                nc.scalar.activation(out_bias[:, :], odd_bank[:, 0:D], ACT.Copy).then_inc(out_bias_ready, 1)

            def normalise1(i, p):
                for t in range(BT):
                    tile = bass.ds(i * BT + t, 1)
                    last = nc.scalar.activation(xn[:, p, t, :], tile_of(x_all, i, t), ACT.Identity,
                                                scale=rstd1[:, tile], bias=shift1[:, tile])
                last.then_inc(xn_done, 1)

            def keep_xn(i, p, source=turn_bank):
                act.wait_ge(xn_turned, i + 1)
                nc.scalar.activation(xn_t[:, p, :], source[:, 0:SEQ], ACT.Copy).then_inc(xn_t_ready, 1)

            def keep_q(i, p, source=query_bank):
                act.wait_ge(q_multiplied, i + 1)
                nc.scalar.activation(q_t[:, p, :], source[:, 0:SEQ], ACT.Identity, scale=SCALE,
                                     bias=q_bias[:, 0:1]).then_inc(q_ready, 1)

            def keep_vo(i, p, source=probs_bank):
                act.wait_ge(vo_multiplied, i + 1)
                nc.scalar.activation(vo[:, p, :, :],
                                     source[:, 0:BT * (D + 1)].rearrange("p (t n) -> p t n", t=BT),
                                     ACT.Copy).then_inc(vo_ready, 1)

            def exponents(i, p, source=score_bank, tiles=range(BT)):
                act.wait_ge(bias_done, i + 1)
                for t in tiles:
                    last = nc.scalar.activation(probs[:, p, t, :], source[:, cols(t, SEQ)], ACT.Exp,
                                                bias=exp_bias[:, p, t:t + 1], accum_out=row_sum[:, p, t:t + 1])
                if t == BT - 1:
                    last.then_inc(exp_done, 1)

            def keep_probs(i, p, source=probs_bank):
                act.wait_ge(probs_turned, i + 1)
                nc.scalar.activation(probs_t[:, p, :, :], source[:, :].rearrange("p (j i) -> p j i", j=BT),
                                     ACT.Copy).then_inc(probs_t_ready, 1)

            def keep_xm(j, p):
                act.wait_ge(xm_turned, j + 1)
                nc.scalar.activation(xm_t[:, p, :], turn_bank[:, 0:SEQ], ACT.Copy).then_inc(xm_t_ready, 1)

            def exp_of_top(j, p):
                act.wait_ge(top_done, j + 1)
                nc.scalar.activation(exp_top[:, p, :], top[:, p, :], ACT.Exp, scale=-1.0).then_inc(top_exp_done, 1)

            def weigh_xm(j, p):
                act.wait_ge(route_w_done, j + 1)
                for t in range(BT):
                    last = nc.scalar.activation(xs[:, p, t, :], xm[:, p, t, :], ACT.Copy,
                                                scale=route_w[:, p, t:t + 1])
                last.then_inc(xs_done, 1)

            def keep_unrouted(j, p):
                act.wait_ge(unrouted_turned, j + 1)
                nc.scalar.activation(unrouted_t[:, p, :], query_bank[0:EXPERTS, 0:SEQ], ACT.Copy
                                     ).then_inc(unrouted_t_ready, 1)

            def round_xs(j, p):
                act.wait_ge(xs_turned, j + 1)
                nc.scalar.activation(xs_hi[:, p, :], turn_bank[:, 0:SEQ], ACT.Copy).then_inc(xs_hi_ready, 1)

            def tanh_of_gate(h, c, banks=loop_banks):
                act.wait_ge(gate_up_done, CHUNKS * h + c + 1)
                if c >= 2 or banks is wide_banks:
                    act.wait_ge(silu_done, CHUNKS * h + c - 1)
                nc.scalar.activation(tanh_g[:, c % 2, :], banks[c][:, 0:SEQ], ACT.Tanh, scale=0.5
                                     ).then_inc(tanh_done, 1)

            def round_weights():
                act.wait_ge(gate_up_in, 16)
                nc.scalar.activation(gate_up_hi[:, :, :, :], gate_up[:, :, :, :], ACT.Copy).then_inc(split_hi, 1)

            keep_vo_product()
            keep_xn(0, 0)
            keep_qk_bias()
            keep_xn(1, 1, attn_bank)
            keep_q(0, 0)
            keep_vo(0, 0)
            round_weights()
            keep_q(1, 1, turn_bank)
            exponents(0, 0)
            keep_out_bias()
            keep_vo(1, 1, attn_bank)
            keep_xn(2, 0, even_bank)
            keep_probs(0, 0)
            keep_q(2, 0, odd_bank)
            exponents(1, 1, down_bank)
            keep_xn(3, 1, probs_bank)
            keep_q(3, 1, odd_bank)
            keep_probs(1, 1, query_bank)
            keep_vo(2, 0, turn_bank)
            exponents(2, 0, even_bank)
            act.wait_ge(attended, 2)
            keep_vo(3, 1, attn_bank)
            keep_xm(0, 0)
            keep_probs(2, 0, odd_bank)
            exponents(3, 1, probs_bank)
            exp_of_top(0, 0)
            weigh_xm(0, 0)
            keep_probs(3, 1, attn_bank)
            round_xs(0, 0)
            keep_unrouted(0, 0)
            keep_xn(LOOPED, 0, query_bank)
            act.wait_ge(shift1_done, 1)

            def one_pass(i, j, h, p):
                q = 1 - p
                keep_xm(j, q)
                tanh_of_gate(h, 0)
                keep_q(i, p)
                exp_of_top(j, q)
                keep_vo(i, p)
                normalise1(i + 1, q)
                tanh_of_gate(h, 1)
                exponents(i, p, tiles=[0])
                tanh_of_gate(h, 2)
                exponents(i, p, tiles=[1])
                tanh_of_gate(h, 3)
                weigh_xm(j, q)
                keep_probs(i, p)
                keep_xn(i + 1, q, score_bank)
                keep_unrouted(j, q)
                round_xs(j, q)

            with act.Fori(0, PAIRS) as pair:
                for p in range(2):
                    one_pass(pair * 2 + (LOOPED + p), pair * 2 + (LOOPED + p - 3), pair * 2 + p, p)
            keep_xm(LOOPED + 1, 1)
            tanh_of_gate(LOOPED, 0, wide_banks)
            exp_of_top(LOOPED + 1, 1)
            tanh_of_gate(LOOPED, 1, wide_banks)
            for h in range(LOOPED, LAST):
                weigh_xm(h + 1, 1 - h % 2)
                tanh_of_gate(h, 2, wide_banks)
                round_xs(h + 1, 1 - h % 2)
                keep_unrouted(h + 1, 1 - h % 2)
                tanh_of_gate(h, 3, wide_banks)
                tanh_of_gate(h + 1, 0, wide_banks)
                if h + 2 <= LAST:
                    keep_xm(h + 2, h % 2)
                tanh_of_gate(h + 1, 1, wide_banks)
                if h + 2 <= LAST:
                    exp_of_top(h + 2, h % 2)
            tanh_of_gate(LAST, 2, wide_banks)
            tanh_of_gate(LAST, 3, wide_banks)

        @block.vector
        def _(dve):
            nc.vector.memset(eps[:, :], EPS).then_inc(filled, 1)
            nc.vector.memset(half_neg[:, :], -0.5).then_inc(filled, 1)
            nc.vector.memset(ones[:, :], 1.0).then_inc(filled, 1)
            nc.vector.memset(x_all[:, TILES:TILES + BT, :], 0.0)
            nc.vector.memset(rstd1[:, TILES:TILES + BT], 0.0)
            nc.vector.memset(shift1[:, TILES:TILES + BT], 0.0)

            def statistics1(lo, hi):
                for t in range(lo, hi):
                    nc.vector.bn_stats(stats1[:, t, :], x_all[:, t, :]).then_inc(stats1_done, 1)
                for t in range(lo, hi):
                    dve.wait_ge(stats1_done, t + 1)
                    nc.vector.bn_aggr(mv1[:, t, :], stats1[:, t, :]).then_inc(mv1_done, 1)

            def mean_shift(lo, hi):
                dve.wait_ge(rstd1_done, 4)
                nc.vector.scalar_tensor_tensor(out=shift1[:, lo:hi], in0=mv1[:, lo:hi, 0], scalar=-1.0,
                                               in1=rstd1[:, lo:hi], op0=ALU.mult, op1=ALU.mult
                                               ).then_inc(shift1_done, 1)

            def row_shift(i, p):
                dve.wait_ge(vo_ready, i + 1)
                nc.vector.tensor_scalar(shift[:, p, :], vo[:, p, :, D], qk_bias[:, 0:1], None, ALU.add
                                        ).then_inc(shift_done, 1)

            def row_maxima(i, p, source=score_bank):
                dve.wait_ge(scored, i + 1)
                nc.vector.tensor_reduce(neg_max[:, p, :], source[:, :].rearrange("p (t j) -> p t j", t=BT),
                                        AX_X, ALU.max, negate=True).then_inc(max_done, 1)

            def less_shift(i, p):
                dve.wait_ge(shift_done, i + 1)
                dve.wait_ge(max_done, i + 1)
                nc.vector.tensor_tensor(neg_max_less[:, p, :], neg_max[:, p, :], shift[:, p, :], ALU.subtract
                                        ).then_inc(less_done, 1)

            def exponent_bias(i, p):
                dve.wait_ge(less_done, i + 1)
                nc.vector.tensor_tensor(exp_bias[:, p, :], neg_max_less[:, p, :], shift[:, p, :], ALU.add
                                        ).then_inc(bias_done, 1)

            def row_inverse(i, p):
                dve.wait_ge(exp_done, i + 1)
                nc.vector.reciprocal(row_inv[:, p, :], row_sum[:, p, :]).then_inc(row_inv_done, 1)

            def add_attention(i, p, source=attn_bank):
                dve.wait_ge(x_bias_ready, i + 1)
                dve.wait_ge(row_inv_done, i + 1)
                dve.wait_ge(attended, i + 1)
                for t in range(BT):
                    last = nc.vector.scalar_tensor_tensor(
                        out=tile_of(x_mid, i, t), in0=source[:, cols(t)], scalar=row_inv[:, p, t:t + 1],
                        in1=tile_of(x_bias, i, t), op0=ALU.mult, op1=ALU.add)
                last.then_inc(x_mid_done, 1)

            def carry_wait():
                nc.vector.memset(scratch[:, :], 0.0)

            def statistics2(j, p):
                dve.wait_ge(x_mid_done, j + 1)
                carry_wait()
                for t in range(BT):
                    last = nc.vector.bn_stats(stats2[:, p, t, :], tile_of(x_mid, j, t))
                last.then_inc(stats2_done, 1)

            def moments2(j, p):
                dve.wait_ge(stats2_done, j + 1)
                carry_wait()
                for t in range(BT):
                    last = nc.vector.bn_aggr(mv2[:, p, t, :], stats2[:, p, t, :])
                last.then_inc(mv2_done, 1)

            def normalise1(i, p):
                dve.wait_ge(rstd1_done, min(i + 1, 4))
                for t in range(BT):
                    last = nc.vector.tensor_scalar(xn[:, p, t, :], x_all[:, i * BT + t, :],
                                                   mv1[:, i * BT + t, 0:1], rstd1[:, i * BT + t:i * BT + t + 1],
                                                   ALU.subtract, ALU.mult)
                last.then_inc(xn_done, 1)

            def choose_expert(j, p, source=query_bank):
                logits = source[:, 0:BT * EXPERTS].rearrange("p (t e) -> p t e", t=BT)

                def spread(v):
                    return v[:, p, :].rearrange("p (t a) -> p t a", a=1).broadcast_to([P, BT, EXPERTS])
                dve.wait_ge(logits_done, j + 1)
                nc.vector.tensor_reduce(top[:, p, :], logits, AX_X, ALU.max).then_inc(top_done, 1)
                dve.wait_ge(top_done, j + 1)
                nc.vector.tensor_tensor(is_top[:, p, :, :], logits, spread(top), ALU.is_equal
                                        ).then_inc(is_top_done, 1)
                dve.wait_ge(is_top_done, j + 1)
                nc.vector.tensor_tensor(ranked[:, p, :, :], is_top[:, p, :, :], prefer[:, :, :], ALU.mult
                                        ).then_inc(ranked_done, 1)
                dve.wait_ge(ranked_done, j + 1)
                nc.vector.tensor_reduce(first[:, p, :], ranked[:, p, :, :], AX_X, ALU.max).then_inc(first_done, 1)
                dve.wait_ge(first_done, j + 1)
                nc.vector.tensor_tensor(unrouted[:, p, :, :], ranked[:, p, :, :], spread(first), ALU.not_equal
                                        ).then_inc(unrouted_done, 1)

            def one_and_exp_of_top(j, p):
                dve.wait_ge(top_exp_done, j + 1)
                nc.vector.tensor_scalar(exp_top1[:, p, :], exp_top[:, p, :], 1.0, None, ALU.add
                                        ).then_inc(exp_top1_done, 1)

            def weight_of_expert(j, p):
                dve.wait_ge(exp_top1_done, j + 1)
                nc.vector.reciprocal(route_w[:, p, :], exp_top1[:, p, :]).then_inc(route_w_done, 1)

            def rest_of_xs(j, p):
                dve.wait_ge(xs_hi_ready, j + 1)
                nc.vector.tensor_tensor(xs_lo[:, p, :], turn_bank[:, 0:SEQ], xs_hi[:, p, :].bitcast(F32),
                                        ALU.subtract).then_inc(xs_lo_ready, 1)

            def hidden(h, p, c, banks=loop_banks):
                gate_up_bank = banks[c]
                dve.wait_ge(tanh_done, CHUNKS * h + c + 1)
                nc.vector.scalar_tensor_tensor(out=silu2[:, c % 2, :], in0=tanh_g[:, c % 2, :], scalar=1.0,
                                               in1=gate_up_bank[:, 0:SEQ], op0=ALU.add, op1=ALU.mult
                                               ).then_inc(silu_done, 1)
                dve.wait_ge(silu_done, CHUNKS * h + c + 1)
                nc.vector.scalar_tensor_tensor(out=hid_t[:, p, c, :], in0=gate_up_bank[:, SEQ:2 * SEQ], scalar=0.5,
                                               in1=silu2[:, c % 2, :], op0=ALU.mult, op1=ALU.mult
                                               ).then_inc(hid_done, 1)

            def add_last_experts():
                for t, source in enumerate(last_down_banks):
                    dve.wait_ge(down_done, BATCHES + t)
                    nc.vector.tensor_tensor(y_all[:, TILES - BT + t, :], source[:, cols(t)],
                                            x_mid[:, TILES - BT + t, :], ALU.add).then_inc(y_done, 1)

            def add_experts(h):
                dve.wait_ge(down_done, h + 1)
                nc.vector.tensor_tensor(batch_tiles(y_all, h),
                                        down_bank[:, 0:BT * D].rearrange("p (t d) -> p t d", t=BT),
                                        batch_tiles(x_mid, h), ALU.add).then_inc(y_done, 1)

            def keep_m():
                dve.wait_ge(m_multiplied, 1)
                nc.vector.tensor_copy(m_sb[:, :], even_bank[:, 0:D]).then_inc(m_ready, 1)
                nc.vector.tensor_scalar(q_bias[:, :], even_bank[:, D:D + 1], SCALE, None, ALU.mult
                                        ).then_inc(m_ready, 1)

            dve.wait_ge(x_first_in, 16)
            statistics1(0, BT)
            statistics1(BT, AHEAD)
            dve.wait_ge(attn_in, 16)
            nc.vector.tensor_copy(bv_wide[:, :], attn_sb[:, BV:BV + 1].broadcast_to([P, P])).then_inc(wide_set, 1)
            nc.vector.tensor_copy(bq_wide[:, :], attn_sb[:, BQ:BQ + 1].broadcast_to([P, P])).then_inc(wide_set, 1)
            normalise1(0, 0)
            keep_m()
            normalise1(1, 1)
            dve.wait_ge(x_rest_in, 16)
            statistics1(AHEAD, AHEAD + BT)
            statistics1(AHEAD + BT, TILES)
            dve.wait_ge(qk_bias_ready, 1)
            row_shift(0, 0)
            row_maxima(0, 0)
            less_shift(0, 0)
            exponent_bias(0, 0)
            normalise1(2, 0)
            row_maxima(1, 1, down_bank)
            row_shift(1, 1)
            less_shift(1, 1)
            exponent_bias(1, 1)
            mean_shift(LOOPED * BT, TILES)
            normalise1(3, 1)
            row_inverse(0, 0)
            add_attention(0, 0)
            statistics2(0, 0)
            moments2(0, 0)
            row_inverse(1, 1)
            row_maxima(2, 0, even_bank)
            row_shift(2, 0)
            less_shift(2, 0)
            exponent_bias(2, 0)
            dve.wait_ge(rstd2_done, 1)
            for t in range(BT):
                last = nc.vector.tensor_scalar(xm[:, 0, t, :], x_mid[:, t, :], mv2[:, 0, t, 0:1],
                                               rstd2[:, 0, t:t + 1], ALU.subtract, ALU.mult)
            last.then_inc(xm_done, 1)
            add_attention(1, 1, score_bank)
            row_maxima(3, 1, probs_bank)
            row_shift(3, 1)
            less_shift(3, 1)
            exponent_bias(3, 1)
            statistics2(1, 1)
            moments2(1, 1)
            dve.wait_ge(prefer_set, 1)
            choose_expert(0, 0)
            one_and_exp_of_top(0, 0)
            weight_of_expert(0, 0)
            row_inverse(2, 0)
            add_attention(2, 0, down_bank)
            rest_of_xs(0, 0)
            statistics2(2, 0)
            moments2(2, 0)
            row_inverse(3, 1)
            add_attention(3, 1, score_bank)

            with dve.Fori(0, PAIRS) as pair:
                for p in range(2):
                    i, j, h, q = pair * 2 + (LOOPED + p), pair * 2 + (LOOPED + p - 3), pair * 2 + p, 1 - p
                    hidden(h, p, 0)
                    choose_expert(j, q, attn_bank)
                    row_maxima(i, p)
                    row_shift(i, p)
                    one_and_exp_of_top(j, q)
                    less_shift(i, p)
                    weight_of_expert(j, q)
                    exponent_bias(i, p)
                    hidden(h, p, 1)
                    hidden(h, p, 2)
                    hidden(h, p, 3)
                    row_inverse(i, p)
                    rest_of_xs(j, q)
                    statistics2(i - 1, q)
                    moments2(i - 1, q)
                    add_attention(i, p)
                    add_experts(h)
            choose_expert(LOOPED + 1, 1)
            one_and_exp_of_top(LOOPED + 1, 1)
            weight_of_expert(LOOPED + 1, 1)
            hidden(LOOPED, 0, 0, wide_banks)
            for h in range(LOOPED, LAST):
                hidden(h, h % 2, 1, wide_banks)
                if h > LOOPED:
                    add_experts(h - 1)
                rest_of_xs(h + 1, 1 - h % 2)
                hidden(h, h % 2, 2, wide_banks)
                hidden(h, h % 2, 3, wide_banks)
                if h == LOOPED:
                    statistics2(LAST, 1)
                    moments2(LAST, 1)
                hidden(h + 1, 1 - h % 2, 0, wide_banks)
                if h + 2 <= LAST:
                    choose_expert(h + 2, h % 2)
                    one_and_exp_of_top(h + 2, h % 2)
                    weight_of_expert(h + 2, h % 2)
            hidden(LAST, 1, 1, wide_banks)
            hidden(LAST, 1, 2, wide_banks)
            hidden(LAST, 1, 3, wide_banks)
            add_experts(LAST - 1)
            add_last_experts()

        @block.tensor
        def _(pe):
            wq, wk, wv, wo_t = (attn_sb[:, w:w + D] for w in (WQ, WK, WV, WOT))

            def warm_up(count):
                for _ in range(count):
                    nc.tensor.transpose(turn_bank[:, 0:P], ident[:, :], ident[:, :])

            def m_product():
                pe.wait_ge(attn_in, 16)
                nc.tensor.matmul(even_bank[:, 0:D], wq, wk, start=True, stop=True)
                nc.tensor.matmul(even_bank[:, D:D + 1], wk, attn_sb[:, BQ:BQ + 1], start=True, stop=True
                                 ).then_inc(m_multiplied, 1)

            def vo_product():
                nc.tensor.matmul(odd_bank[:, 0:D], wv, wo_t, start=True, stop=True)
                nc.tensor.matmul(odd_bank[:, D:D + 1], wq, attn_sb[:, BK:BK + 1], start=True, stop=True
                                 ).then_inc(vo_w_multiplied, 1)

            def qk_bias_product():
                pe.wait_ge(m_ready, 2)
                pe.wait_ge(wide_set, 2)
                nc.tensor.matmul(even_bank[:, 0:1], bq_wide[:, :], attn_sb[:, BK:BK + 1], start=True, stop=True
                                 ).then_inc(qk_bias_multiplied, 1)

            def out_bias_product():
                pe.wait_ge(vo_w_ready, 1)
                nc.tensor.matmul(odd_bank[:, 0:D], bv_wide[:, :], wo_t, start=True, stop=False)
                pe.wait_ge(filled, 3)
                pe.wait_ge(bo_in, 16)
                nc.tensor.matmul(odd_bank[:, 0:D], ones[0:1, :], bo_row[:, :], start=False, stop=True
                                 ).then_inc(out_bias_multiplied, 1)

            def turn(source, p, done, target=turn_bank):
                for t in range(BT):
                    last = nc.tensor.transpose(target[:, cols(t)], source[:, p, t, :], ident[:, :])
                last.then_inc(done, 1)

            def turn_xn(i, p, target=turn_bank):
                pe.wait_ge(xn_done, i + 1)
                turn(xn, p, xn_turned, target)

            def query(i, p, target=query_bank):
                pe.wait_ge(xn_t_ready, i + 1)
                nc.tensor.matmul(target[:, 0:SEQ], m_sb[:, :], xn_t[:, p, :], start=True, stop=True
                                 ).then_inc(q_multiplied, 1)

            def value(i, p, target=probs_bank):
                pe.wait_ge(xn_t_ready, i + 1)
                for t in range(BT):
                    last = nc.tensor.matmul(target[:, cols(t, D + 1)], xn_t[:, p, cols(t)], vo_sb[:, :],
                                            start=True, stop=True)
                last.then_inc(vo_multiplied, 1)

            def scores(i, p, target=score_bank):
                pe.wait_ge(q_ready, i + 1)
                for t in range(BT):
                    last = nc.tensor.matmul(target[:, cols(t, SEQ)], q_t[:, p, cols(t)], xn_t[:, p, :],
                                            start=True, stop=True)
                last.then_inc(scored, 1)

            def turn_probs(i, p, target=probs_bank):
                pe.wait_ge(vo_ready, i + 1)
                pe.wait_ge(exp_done, i + 1)
                for j in range(BT):
                    for t in range(BT):
                        last = nc.tensor.transpose(target[:, j * SEQ + t * P:j * SEQ + (t + 1) * P],
                                                   probs[:, p, t, cols(j)], ident[:, :])
                last.then_inc(probs_turned, 1)

            def attend(i, p, target=attn_bank):
                pe.wait_ge(probs_t_ready, i + 1)
                for t in range(BT):
                    for j in range(BT):
                        last = nc.tensor.matmul(target[:, cols(t)], probs_t[:, p, j, cols(t)],
                                                vo[:, p, j, 0:D], start=(j == 0), stop=(j == BT - 1))
                last.then_inc(attended, 1)

            def turn_xm(j, p):
                pe.wait_ge(xm_done, j + 1)
                turn(xm, p, xm_turned)

            def logits(j, p, target=query_bank):
                pe.wait_ge(xm_t_ready, j + 1)
                for t in range(BT):
                    last = nc.tensor.matmul(target[:, cols(t, EXPERTS)], xm_t[:, p, cols(t)],
                                            router_w[:, :], start=True, stop=True)
                last.then_inc(logits_done, 1)

            def turn_unrouted(j, p):
                pe.wait_ge(unrouted_done, j + 1)
                for t in range(BT):
                    last = nc.tensor.transpose(query_bank[0:EXPERTS, cols(t)], unrouted[:, p, t, :], ident[:, :])
                last.then_inc(unrouted_turned, 1)

            def turn_xs(j, p):
                pe.wait_ge(xs_done, j + 1)
                turn(xs, p, xs_turned)

            def gate_and_up(h, p, c, banks=loop_banks):
                target = banks[c]
                if c == 0:
                    pe.wait_ge(xs_lo_ready, h + 1)
                    pe.wait_ge(unrouted_t_ready, h + 1)
                if banks is wide_banks:
                    pe.wait_ge(hid_done, max(CHUNKS * LOOPED, CHUNKS * h + c + 1 - CHUNKS))
                elif banks[c] in banks[:c]:
                    pe.wait_ge(hid_done, CHUNKS * h + banks.index(banks[c]) + 1)
                for which in range(2):
                    half = target[:, cols(which, SEQ)]
                    w_hi, w_lo = gate_up_hi[:, which, c, :], gate_up_lo[:, which, c, :]
                    if which == 0:
                        nc.tensor.matmul(half, penalty[:, c, :, :].rearrange("e s i -> e (s i)"),
                                         unrouted_t[:, p, :], start=True, stop=False)
                    nc.tensor.matmul(half, w_lo, xs_hi[:, p, :], start=(which == 1), stop=False)
                    nc.tensor.matmul(half, w_hi, xs_lo[:, p, :], start=False, stop=False)
                    last = nc.tensor.matmul(half, w_hi, xs_hi[:, p, :], start=False, stop=True)
                last.then_inc(gate_up_done, 1)

            def down(h, p, t, chunks, target=down_bank):
                pe.wait_ge(hid_done, CHUNKS * h + chunks[-1] + 1)
                for c in chunks:
                    last = nc.tensor.matmul(target[:, cols(t)], hid_t[:, p, c, cols(t)], down_w[:, c, :],
                                            start=(c == 0), stop=(c == CHUNKS - 1))
                if c == CHUNKS - 1 and (t == BT - 1 or target is not down_bank):
                    last.then_inc(down_done, 1)

            every = list(range(CHUNKS))
            pe.wait_ge(ident_set, 2)
            warm_up(14)
            m_product()
            vo_product()
            warm_up(4)
            turn_xn(0, 0)
            qk_bias_product()
            turn_xn(1, 1, attn_bank)
            query(0, 0)
            pe.wait_ge(vo_w_ready, 1)
            value(0, 0)
            scores(0, 0)
            query(1, 1, turn_bank)
            value(1, 1, attn_bank)
            out_bias_product()
            scores(1, 1, down_bank)
            pe.wait_ge(qk_bias_ready, 1)
            turn_xn(2, 0, even_bank)
            turn_probs(0, 0)
            pe.wait_ge(out_bias_ready, 1)
            query(2, 0, odd_bank)
            value(2, 0, turn_bank)
            attend(0, 0)
            turn_xn(3, 1, probs_bank)
            scores(2, 0, even_bank)
            query(3, 1, odd_bank)
            turn_probs(1, 1, query_bank)
            pe.wait_ge(x_mid_done, 1)
            value(3, 1, attn_bank)
            attend(1, 1, score_bank)
            scores(3, 1, probs_bank)
            pe.wait_ge(vo_ready, 3)
            turn_xm(0, 0)
            turn_probs(2, 0, odd_bank)
            pe.wait_ge(router_in, 16)
            logits(0, 0)
            attend(2, 0, down_bank)
            turn_probs(3, 1, attn_bank)
            turn_unrouted(0, 0)
            turn_xs(0, 0)
            pe.wait_ge(x_mid_done, 2)
            attend(3, 1, score_bank)
            pe.wait_ge(unrouted_t_ready, 1)
            turn_xn(LOOPED, 0, query_bank)
            pe.wait_ge(split_ready, 1)
            pe.wait_ge(penalty_set, 2)
            pe.wait_ge(down_in, 16)

            with pe.Fori(0, PAIRS) as pair:
                for p in range(2):
                    i, j, h, q = pair * 2 + (LOOPED + p), pair * 2 + (LOOPED + p - 3), pair * 2 + p, 1 - p
                    pe.wait_ge(xs_lo_ready, h + 1)
                    turn_xm(j, q)
                    gate_and_up(h, p, 0)
                    query(i, p)
                    pe.wait_ge(x_mid_done, i)
                    logits(j, q, attn_bank)
                    value(i, p)
                    scores(i, p)
                    gate_and_up(h, p, 1)
                    pe.wait_ge(is_top_done, j + 1)
                    gate_and_up(h, p, 2)
                    gate_and_up(h, p, 3)
                    down(h, p, 0, [0, 1])
                    turn_probs(i, p)
                    turn_xn(i + 1, q, score_bank)
                    down(h, p, 0, [2])
                    turn_xs(j, q)
                    turn_unrouted(j, q)
                    down(h, p, 0, [3])
                    attend(i, p)
                    down(h, p, 1, every)
            pe.wait_ge(xn_t_ready, BATCHES + 1)
            pe.wait_ge(xs_lo_ready, LOOPED + 1)
            turn_xm(LOOPED + 1, 1)
            gate_and_up(LOOPED, 0, 0, wide_banks)
            logits(LOOPED + 1, 1)
            gate_and_up(LOOPED, 0, 1, wide_banks)
            for h in range(LOOPED, LAST):
                gate_and_up(h, h % 2, 2, wide_banks)
                gate_and_up(h, h % 2, 3, wide_banks)
                turn_xs(h + 1, 1 - h % 2)
                turn_unrouted(h + 1, 1 - h % 2)
                pe.wait_ge(y_done, h)
                down(h, h % 2, 0, every[:2])
                gate_and_up(h + 1, 1 - h % 2, 0, wide_banks)
                if h + 2 <= LAST:
                    turn_xm(h + 2, h % 2)
                    down(h, h % 2, 0, every[2:-1])
                    gate_and_up(h + 1, 1 - h % 2, 1, wide_banks)
                    logits(h + 2, h % 2)
                    down(h, h % 2, 0, every[-1:])
                    down(h, h % 2, 1, every)
            down(LAST - 1, 0, 0, every[2:-1])
            gate_and_up(LAST, 1, 1, wide_banks)
            down(LAST - 1, 0, 0, every[-1:])
            gate_and_up(LAST, 1, 2, wide_banks)
            gate_and_up(LAST, 1, 3, wide_banks)
            down(LAST - 1, 0, 1, every)
            for c in every:
                for t, target in enumerate(last_down_banks):
                    down(LAST, 1, t, [c], target)


def kernel(**inputs):
    import numpy as np
    import concourse.bacc as bacc
    from concourse.bass_utils import run_bass_kernel_spmd

    def f32(name):
        return np.asarray(inputs[name])

    def column(name):
        return f32(name).reshape(D, 1)

    arrays = {
        "x": f32("L0_attn_x"),
        "attn_w": np.concatenate([f32("L0_attn_w_q"), f32("L0_attn_w_k"), f32("L0_attn_w_v"), f32("L0_attn_w_out").T,
                                  column("L0_attn_b_q"), column("L0_attn_b_k"), column("L0_attn_b_v")], axis=1),
        "bo": f32("L0_attn_b_out").reshape(1, D),
        "gate_up_t": np.concatenate([f32("L0_ffn_w_gate").reshape(EXPERTS * HIDDEN, D).T,
                                     f32("L0_ffn_w_up").reshape(EXPERTS * HIDDEN, D).T], axis=1),
        "down_t": f32("L0_ffn_w_down").transpose(0, 2, 1).reshape(EXPERTS * HIDDEN, D),
        "router_t": f32("L0_ffn_gate_w").T,
    }
    nc = bacc.Bacc("TRN2", target_bir_lowering=False, num_devices=1)
    sent, args = {}, []
    for name, a in arrays.items():
        a = np.ascontiguousarray(a)
        sent[f"in_{name}"] = a
        args.append(nc.dram_tensor(f"in_{name}", a.shape, mybir.dt.from_np(a.dtype), kind="ExternalInput").ap())
    out = nc.dram_tensor("out_x", [BATCHES, SEQ, D], F32, kind="ExternalOutput").ap()
    layer_kernel(nc, *args, out)
    result = run_bass_kernel_spmd(nc, [sent], core_ids=[0])
    return result.results[0]["out_x"]
```
